# Optimizing a Trainium2 kernel written in Bass

```python
import numpy as np
import jax
import jax.numpy as jnp

def _softmax(x, axis=-1):
    return jax.nn.softmax(x, axis=axis)
def _gelu(x):
    return jax.nn.gelu(x, approximate=True)
def _silu(x):
    return jax.nn.silu(x)
def _sigmoid(x):
    return jax.nn.sigmoid(x)
def _layernorm(x, axis=-1, eps=1e-5):
    m = jnp.mean(x, axis=axis, keepdims=True)
    v = jnp.var(x, axis=axis, keepdims=True)
    return (x - m) / jnp.sqrt(v + eps)
def _scatter_add(tgt, idx, src, axis=0):
    return tgt.at[idx].add(src)
def _segment_sum(src, seg, n):
    return jax.ops.segment_sum(src, seg, n)

kernel_name = 'mk_conv_preact_d2_conv_nchw64_a2129e'

def setup_inputs(seed: int = 0):
    np.random.seed(seed)
    _w = jnp.asarray
    def _rec_inputs():
        import jax
        import jax.numpy as jnp
        _gk = jax.random.key(seed)
        x = -0.0003929 + 0.9999 * jax.random.normal(jax.random.fold_in(_gk, 1), (16, 64, 128, 128), jnp.float32)
        return x
    x = _rec_inputs()
    def _L0_conv_setup():
        import jax, jax.numpy as jnp
        import numpy as np
        B, CIN, COUT, H, W, K = (16, 64, 64, 128, 128, 3)

        def _circular_pad(weight, n_h, n_w):
            cout, cin, kh, kw = weight.shape
            ph, pw = (kh // 2, kw // 2)
            w = jnp.flip(weight, axis=(-2, -1))
            w = jnp.pad(w, ((0, 0), (0, 0), (0, n_h - kh), (0, n_w - kw)))
            return jnp.roll(w, shift=(-ph, -pw), axis=(-2, -1))
        key = jax.random.key(seed)
        k1, k2 = jax.random.split(key)
        x = jax.random.normal(k1, (B, CIN, H, W), dtype=jnp.float32)
        weight = jax.random.normal(k2, (COUT, CIN, K, K), dtype=jnp.float32)
        weight = weight * np.float32(np.sqrt(2.0 / (CIN * K * K)))
        return {'x': x, 'weight': weight}
    _L0_conv_all = _L0_conv_setup()
    _L0_conv_in = {k: v for k, v in _L0_conv_all.items() if k in ('weight', )}
    del _L0_conv_all

    def _L1_conv_setup():
        import jax, jax.numpy as jnp
        import numpy as np
        K_MAX = 5
        PATCH = 4
        DIAG_EPS = 1e-05
        EPS = 1e-10

        def batch_omp(X, D):
            M, B = X.shape
            N = D.shape[1]
            G = D.T @ D + DIAG_EPS * jnp.eye(N, dtype=X.dtype)
            h_bar = (D.T @ X).T
            h = h_bar
            x_stack = None
            L = jnp.ones((B, 1, 1), X.dtype)
            I = jnp.zeros((B, 0), jnp.int32)
            mask = jnp.zeros((B, N), bool)
            bidx = jnp.arange(B)
            for k in range(1, K_MAX + 1):
                scores = jnp.abs(h * (~mask).astype(h.dtype))
                index = jnp.argmax(scores, axis=1).astype(jnp.int32)
                mask = mask.at[bidx, index].set(True)
                if k > 1:
                    G_stack = G[I, index[:, None]]
                    w = jax.scipy.linalg.solve_triangular(L, G_stack[..., None], lower=True)[..., 0]
                    w_corner = jnp.sqrt(jnp.clip(1.0 - jnp.sum(w * w, axis=1, keepdims=True), DIAG_EPS))
                    top = jnp.concatenate([L, jnp.zeros((B, k - 1, 1), X.dtype)], axis=2)
                    bot = jnp.concatenate([w, w_corner], axis=1)[:, None, :]
                    L = jnp.concatenate([top, bot], axis=1)
                I = jnp.concatenate([I, index[:, None]], axis=1)
                h_stack = jnp.take_along_axis(h_bar, I, axis=1)[..., None]
                y = jax.scipy.linalg.solve_triangular(L, h_stack, lower=True)
                x_stack = jax.scipy.linalg.solve_triangular(jnp.swapaxes(L, -1, -2), y, lower=False)[..., 0]
                beta = jnp.einsum('bk,bkn->bn', x_stack, G[I])
                h = h_bar - beta
            coeffs = jnp.zeros((B, N), X.dtype).at[bidx[:, None], I].set(x_stack)
            return coeffs.T
        key = jax.random.key(seed)
        k1, k2 = jax.random.split(key)
        z = jax.random.normal(k1, (32, 64, 128, 128), dtype=jnp.float32)
        dictionary = jax.random.normal(k2, (1024, 512), dtype=jnp.float32)
        return {'z': z, 'dictionary': dictionary}
    _L1_conv_all = _L1_conv_setup()
    _L1_conv_in = {k: v for k, v in _L1_conv_all.items() if k in ('dictionary', )}
    del _L1_conv_all

    return {
        "x": x,
        "L0_conv_weight": _L0_conv_in["weight"],
        "L1_conv_dictionary": _L1_conv_in["dictionary"],
    }

def reference(x, L0_conv_weight, L1_conv_dictionary):
    import jax
    import jax.numpy as jnp
    def _L0_conv_ref(x, weight):
        import jax, jax.numpy as jnp
        import numpy as np
        B, CIN, COUT, H, W, K = (16, 64, 64, 128, 128, 3)

        def _circular_pad(weight, n_h, n_w):
            cout, cin, kh, kw = weight.shape
            ph, pw = (kh // 2, kw // 2)
            w = jnp.flip(weight, axis=(-2, -1))
            w = jnp.pad(w, ((0, 0), (0, 0), (0, n_h - kh), (0, n_w - kw)))
            return jnp.roll(w, shift=(-ph, -pw), axis=(-2, -1))
        _, _, n_h, n_w = x.shape
        w_pad = _circular_pad(weight, n_h, n_w)
        x_f = jnp.fft.fft2(x)
        w_f = jnp.fft.fft2(w_pad)
        y_f = jnp.einsum('bihw,oihw->bohw', x_f, w_f)
        y = jnp.real(jnp.fft.ifft2(y_f))
        return y.astype(x.dtype)

    def _L1_conv_ref(z, dictionary):
        import jax, jax.numpy as jnp
        import numpy as np
        K_MAX = 5
        PATCH = 4
        DIAG_EPS = 1e-05
        EPS = 1e-10

        def batch_omp(X, D):
            M, B = X.shape
            N = D.shape[1]
            G = D.T @ D + DIAG_EPS * jnp.eye(N, dtype=X.dtype)
            h_bar = (D.T @ X).T
            h = h_bar
            x_stack = None
            L = jnp.ones((B, 1, 1), X.dtype)
            I = jnp.zeros((B, 0), jnp.int32)
            mask = jnp.zeros((B, N), bool)
            bidx = jnp.arange(B)
            for k in range(1, K_MAX + 1):
                scores = jnp.abs(h * (~mask).astype(h.dtype))
                index = jnp.argmax(scores, axis=1).astype(jnp.int32)
                mask = mask.at[bidx, index].set(True)
                if k > 1:
                    G_stack = G[I, index[:, None]]
                    w = jax.scipy.linalg.solve_triangular(L, G_stack[..., None], lower=True)[..., 0]
                    w_corner = jnp.sqrt(jnp.clip(1.0 - jnp.sum(w * w, axis=1, keepdims=True), DIAG_EPS))
                    top = jnp.concatenate([L, jnp.zeros((B, k - 1, 1), X.dtype)], axis=2)
                    bot = jnp.concatenate([w, w_corner], axis=1)[:, None, :]
                    L = jnp.concatenate([top, bot], axis=1)
                I = jnp.concatenate([I, index[:, None]], axis=1)
                h_stack = jnp.take_along_axis(h_bar, I, axis=1)[..., None]
                y = jax.scipy.linalg.solve_triangular(L, h_stack, lower=True)
                x_stack = jax.scipy.linalg.solve_triangular(jnp.swapaxes(L, -1, -2), y, lower=False)[..., 0]
                beta = jnp.einsum('bk,bkn->bn', x_stack, G[I])
                h = h_bar - beta
            coeffs = jnp.zeros((B, N), X.dtype).at[bidx[:, None], I].set(x_stack)
            return coeffs.T
        """Patch-wise OMP sparse coding bottleneck (forward reconstruction path).
            z: [B, C, H, W]; dictionary: [atom_dim, num_embeddings], atom_dim = C*PATCH^2.
            """
        D = dictionary / (jnp.linalg.norm(dictionary, axis=0, keepdims=True) + EPS)
        B, C, H, W = z.shape
        p = PATCH
        hb, wb = (H // p, W // p)
        patches = z.reshape(B, C, hb, p, wb, p).transpose(0, 2, 4, 1, 3, 5).reshape(B * hb * wb, C * p * p)
        X = patches.T
        coeffs = batch_omp(X, D)
        X_hat = D @ coeffs
        recon = X_hat.T.reshape(B, hb, wb, C, p, p).transpose(0, 3, 1, 4, 2, 5).reshape(B, C, H, W)
        return recon

    def _gn(v, G=32, eps=1e-5):
        B_, C_, H_, W_ = v.shape
        g = v.reshape(B_, G, C_ // G, H_, W_)
        m = jnp.mean(g, axis=(2, 3, 4), keepdims=True)
        s = jnp.var(g, axis=(2, 3, 4), keepdims=True)
        return ((g - m) / jnp.sqrt(s + eps)).reshape(v.shape)

    def _ln_c(v, eps=1e-6):
        m = jnp.mean(v, axis=1, keepdims=True)
        s = jnp.var(v, axis=1, keepdims=True)
        return (v - m) / jnp.sqrt(s + eps)

    def _ln_t(v, eps=1e-5):
        m = jnp.mean(v, axis=-1, keepdims=True)
        s = jnp.var(v, axis=-1, keepdims=True)
        return (v - m) / jnp.sqrt(s + eps)

    def _to_tokens(v):
        B_, C_, H_, W_ = v.shape
        return v.reshape(B_, C_, H_ * W_).transpose(0, 2, 1)
    def _from_tokens(t, like):
        B_, C_, H_, W_ = like.shape
        return t.transpose(0, 2, 1).reshape(B_, C_, H_, W_)

    x = x + _L0_conv_ref(_gn(x), L0_conv_weight)
    x = x + _L1_conv_ref(_gn(x), L1_conv_dictionary)
    return x


_drawn_inputs = setup_inputs


def setup_inputs(seed=0):
    import zlib

    import numpy as np

    out = dict(_drawn_inputs(seed))
    spreads = {}
    factors = {}
    for name, (base, spread) in spreads.items():
        noise = np.random.default_rng([zlib.crc32(name.encode()), seed]).standard_normal(out[name].shape)
        drawn = base * np.exp(spread * noise) if base else spread * noise
        out[name] = jnp.asarray(drawn.astype(out[name].dtype))
    for name, factor in factors.items():
        out[name] = (out[name] * factor).astype(out[name].dtype)
    return out
```

```python
import numpy as np
import concourse.bass as bass
from concourse import mybir
from contextlib import ExitStack

F32 = mybir.dt.float32
F16 = mybir.dt.float16
BF16 = mybir.dt.bfloat16
U32 = mybir.dt.uint32
ALU = mybir.AluOpType
ACT = mybir.ActivationFunctionType
AX = mybir.AxisListType

P = 128
CIN = 64
W = 128
PAIRS = 64
TAPS = 3
PATCH = 4
DIM = CIN * PATCH * PATCH
ND = DIM // P
ATOMS = 512
NA = ATOMS // P
KMAX = 5
T = 4
GROUPS = 2
TILES = T * GROUPS
TP = PAIRS // TILES
CP = 4
CHUNKS = PAIRS // CP
QUARTERS = 4
QP = PAIRS // QUARTERS
XN_RING = 4
SLOTS = GROUPS * KMAX * T
GN_EPS = 1e-5
NORM_EPS = 1e-10
DIAG_EPS = 1e-5
GN_STEPS = 10
PICKS = T * sum(1 + k for k in range(KMAX))
ROWS = T * sum(range(KMAX - 1))
ALG = 1 + 6 * (KMAX - 1) - 1 + 1 + 2 * (KMAX - 1)

VECTOR_PLAN = {
    0: [("ce", 1, 0), ("ce", 1, 1)], 1: [("ce", 1, 2), ("ce", 1, 3), ("xs", 0)], 2: [("xs", 1)], 3: [("ra", 1, 0)],
    4: [("ra", 1, 1), ("ra", 1, 2)], 5: [("ra", 1, 3), ("ra", 1, 4)], 6: [("ra", 1, 5), ("ra", 1, 6)],
    7: [("ra", 1, 7)], 9: [("xs", 2)], 10: [("xs", 3), ("gn", 0, 0)], 11: [("gn", 0, 1)], 12: [("gn", 0, 2)],
    13: [("ca", 0)], 14: [("ca", 1), ("ca", 2)], 15: [("ca", 3), ("ca", 4)], 16: [("ca", 5)],
    17: [("ca", 6), ("ca", 7)], 18: [("ca", 8)], 19: [("ca", 9), ("ca", 10)], 21: [("ca", 11)],
    22: [("ca", 12)], 23: [("ca", 13)], 24: [("ca", 14)],
    25: [("ca", 15), ("ce", 0, 0), ("zs",), ("gn", 1, 0)], 26: [("ce", 0, 1), ("ce", 0, 2)],
    27: [("ce", 0, 3), ("gn", 1, 1)], 28: [("gn", 1, 2)], 29: [("ra", 0, 0)], 30: [("ra", 0, 1), ("ra", 0, 2)],
    31: [("ra", 0, 3)], 32: [("ra", 0, 4), ("ra", 0, 5)], 33: [("ra", 0, 6)], 34: [("ra", 0, 7)],
}
SCALAR_PLAN = {
    1: [("ct", 1, 0), ("ct", 1, 1)], 2: [("ct", 1, 2)], 3: [("ct", 1, 3)],
    4: [("z", 4)], 5: [("z", 5)], 8: [("h", 4), ("z", 6)], 9: [("h", 5), ("z", 7)], 10: [("h", 6)], 11: [("h", 7)],
    12: [("rt", 0)], 13: [("xn", 0), ("xn", 1), ("xn", 2)], 14: [("xn", 3), ("xn", 4)], 15: [("xn", 5), ("xn", 6)],
    16: [("xn", 7)], 17: [("xn", 8), ("xn", 9)], 18: [("xn", 10)], 19: [("xn", 11), ("xn", 12)],
    20: [("xn", 13)], 22: [("xn", 14)], 23: [("xn", 15)],
    26: [("ct", 0, 0)], 27: [("ct", 0, 1), ("ct", 0, 2)], 28: [("ct", 0, 3), ("rt", 1)],
    30: [("z", 0)], 31: [("z", 1)], 35: [("h", 0), ("z", 2)], 36: [("h", 1), ("z", 3)],
    37: [("h", 2)], 38: [("h", 3)],
}
OWN = ("xs", "ca", "zs", "gn", "xn", "rt")


def at(image, per_image, n):
    return image * per_image + n


def preact_conv_pursuit(nc, x, w_taps, atoms, ident_in, avg_in, out):
    images = x.shape[0]
    gram = nc.dram_tensor("gram_rows", (ATOMS, ATOMS), F32).ap()

    ctx = ExitStack()
    with ctx:
        def sb(name, shape, dt=F32):
            return ctx.enter_context(nc.sbuf_tensor(name, shape, dt))

        def sem(name):
            return ctx.enter_context(nc.semaphore(name))

        xa = [sb(f"xa{n}", [P, PAIRS + 2, W]) for n in range(2)]
        xn = sb("xn", [P, XN_RING, CP + 1, W + 2])
        z = sb("z", [P, 2, 2, PATCH, P])
        dn = sb("dn", [P, ND, ATOMS])
        dt_ = sb("dt", [P, NA, ND, P])
        wc = sb("wc", [P, 2 * TAPS, P])
        h = sb("h", [P, TILES, ATOMS])
        u = sb("u", [P, T, KMAX - 1, ATOMS])
        hot = sb("hot", [P, T, ATOMS], BF16)
        mask = sb("mask", [P, T, ATOMS], F16)
        ce = sb("ce", [P, KMAX, ATOMS])
        ct = sb("ct", [P, NA, T * P])
        junk = sb("junk", [P, 4, ATOMS], BF16)
        count = sb("count", [P, ATOMS], F16)
        ident = sb("ident", [P, P])
        avg = sb("avg", [P, P])
        top8 = sb("top8", [P, T, 8])
        idx8 = sb("idx8", [P, T, 8], U32)
        which = sb("which", [P, GROUPS, KMAX, T])
        hsel = sb("hsel", [P, GROUPS, KMAX, T])
        v = sb("v", [P, GROUPS, KMAX, KMAX, T])
        rd = sb("rd", [P, GROUPS, KMAX, T])
        nl = sb("nl", [P, GROUPS, KMAX, KMAX, T])
        na = sb("na", [P, GROUPS, KMAX, T])
        sq = sb("sq", [P, KMAX, T])
        ss = sb("ss", [P, T])
        dd = sb("dd", [P, T])
        xc = sb("xc", [P, GROUPS, KMAX, T])
        tmp = sb("tmp", [P, KMAX, T])
        bn = [sb(f"bn{n}", [P, CHUNKS, 6]) for n in range(2)]
        mv = sb("mv", [P, 2])
        gsc = sb("gsc", [P, 8])
        fac = [sb(f"fac{n}", [P, 2, 2]) for n in range(2)]

        conv_ps = [ctx.enter_context(nc.psum_tensor(f"conv_ps{n}", [P, CP, W], F32)) for n in range(2)]
        gen_ps = [ctx.enter_context(nc.psum_tensor(f"gen_ps{n}", [P, ATOMS], F32)) for n in range(2)]
        ct_ps = ctx.enter_context(nc.psum_tensor("ct_ps", [P, NA, P], F32))
        score = [ctx.enter_context(nc.psum_tensor(f"score{n}", [P, ATOMS], F32)) for n in range(2)]
        st_ps = ctx.enter_context(nc.psum_tensor("st_ps", [P, ATOMS], F32))

        setup(nc, ctx, sem, w_taps, atoms, ident_in, avg_in, gram, dn, dt_, wc, h, u, count, ident, avg,
              rd, gen_ps, ct_ps, st_ps)

        x_loaded = [sem(f"x_loaded{q}") for q in range(QUARTERS)]
        x_edge = [sem(f"x_edge{n}") for n in range(2)]
        vector_passed = sem("vector_passed")
        pool_passed = sem("pool_passed")
        sync_passed = sem("sync_passed")
        out_stored = [sem(f"out_stored{q}") for q in range(QUARTERS)]
        x_stats = sem("x_stats")
        gn_step = sem("gn_step")
        gn_sum = sem("gn_sum")
        gn_root = sem("gn_root")
        xn_ready = sem("xn_ready")
        conv_done = sem("conv_done")
        x1_ready = sem("x1_ready")
        x1_stats = sem("x1_stats")
        z_ready = sem("z_ready")
        corr_done = sem("corr_done")
        h_ready = sem("h_ready")
        h_updated = sem("h_updated")
        h_masked = sem("h_masked")
        score_ready = sem("score_ready")
        top_found = sem("top_found")
        atom_found = sem("atom_found")
        which_ready = sem("which_ready")
        hot_ready = sem("hot_ready")
        mask_ready = sem("mask_ready")
        picked = sem("picked")
        alg_step = sem("alg_step")
        row_step = sem("row_step")
        row_loaded = [sem(f"row_loaded{t}") for t in range(T)]
        ce_ready = sem("ce_ready")
        ce_turned = sem("ce_turned")
        ct_ready = sem("ct_ready")
        recon_done = sem("recon_done")
        recon_added = sem("recon_added")

        LATER = SLOTS - GROUPS * T

        def loaded(eng, q, image, par):
            eng.dma_start(xa[par][:, 1 + q * QP:1 + (q + 1) * QP, :], x[image][:, q * QP:(q + 1) * QP, :])\
                .then_inc(x_loaded[q], 16)
            if q == 0:
                eng.dma_start(xa[par][:, PAIRS + 1, :], x[image][:, 0, :]).then_inc(x_edge[0], 16)
            if q == QUARTERS - 1:
                eng.dma_start(xa[par][:, 0, :], x[image][:, PAIRS - 1, :]).then_inc(x_edge[1], 16)

        def periods(eng, period):
            period(0, 0)
            period(1, 1)
            with eng.Fori(0, (images - 2) // 2) as j:
                period(j * 2 + 2, 0, True)
                period(j * 2 + 3, 1, True)
            period(images, 0)
            period(images + 1, 1)

        def parts(i, loop):
            if loop:
                return True, True, True
            return i < images, 1 <= i <= images, i >= 2

        block = ctx.enter_context(nc.Block())

        @block.sync
        def _(sp):
            for q in range(QUARTERS):
                loaded(sp, q, 0, 0)
            sp.wait_ge(x_edge[0], 16)
            for q in range(QUARTERS // 2):
                sp.wait_ge(x_loaded[q], 16)
                loaded(sp, q, 1, 1)

            def stop_until(sem_, value):
                sp.wait_ge(sem_, value)
                sp.sem_inc(sync_passed, 1)

            def period(i, par, loop=False):
                own, b, p = parts(i, loop)
                if p:
                    stop_until(recon_added, at(i, 2 * ND, -2 * ND))
                    for q in (2, 3):
                        sp.dma_start(out[i - 2][:, q * QP:(q + 1) * QP, :], xa[par][:, 1 + q * QP:1 + (q + 1) * QP, :])\
                            .then_inc(out_stored[q], 16)
                if own:
                    for q in (2, 3):
                        if p:
                            stop_until(out_stored[q], at(i, 16, -16))
                        elif i == 1:
                            stop_until(x_loaded[q], 16)
                            if q == QUARTERS - 1:
                                stop_until(x_edge[1], 16)
                        if not (isinstance(i, int) and i == 0):
                            loaded(sp, q, i, par)
                if b:
                    stop_until(recon_added, at(i, 2 * ND, -ND))
                    for q in (0, 1):
                        sp.dma_start(out[i - 1][:, q * QP:(q + 1) * QP, :],
                                     xa[1 - par][:, 1 + q * QP:1 + (q + 1) * QP, :]).then_inc(out_stored[q], 16)
                    if loop or i + 1 < images:
                        for q in (0, 1):
                            stop_until(out_stored[q], at(i, 16, 0))
                            loaded(sp, q, i + 1, 1 - par)

            period(0, 0)
            period(1, 1)
            with sp.Fori(0, (images - 4) // 2) as j:
                period(j * 2 + 2, 0, True)
                period(j * 2 + 3, 1, True)
            for i in range(images - 2, images + 2):
                period(i, i % 2)
            for q in range(QUARTERS):
                sp.wait_ge(out_stored[q], 16 * images)

        @block.gpsimd
        def _(pool):
            def period(i, par, loop=False):
                _, b, _ = parts(i, loop)
                if not b:
                    return
                img = i - 1
                for g in range(GROUPS):
                    for k in range(KMAX):
                        for t in range(T):
                            if k > 0:
                                n = (g * (KMAX - 1) + k - 1) * T + t
                                pool.wait_ge(h_updated, at(img, LATER, n + 1))
                                pool.tensor_tensor(h[:, g * T + t, :], h[:, g * T + t, :], mask[:, t, :], ALU.mult)\
                                    .then_inc(h_masked, 1)
                        for t in range(T if k < KMAX - 1 else 0):
                            n = (g * KMAX + k) * T + t
                            pool.wait_ge(atom_found, at(img, SLOTS, n + 1))
                            pool.sem_inc(pool_passed, 1)
                            pool.indirect_dma_start(u[:, t, k, :], None, gram,
                                                    bass.IndirectOffsetOnAxis(ap=idx8[:, t, 0:1], axis=0))\
                                .then_inc(row_loaded[t], 16)

            periods(pool, period)

        @block.scalar
        def _(act):
            def extra(what, i, par):
                kind, *a = what
                if kind == "ct":
                    g, t = a
                    img = i - 2 if g else i - 1
                    n = g * T + t
                    act.wait_ge(ce_turned, at(img, TILES * KMAX, (n + 1) * KMAX))
                    if not (isinstance(img, int) and img == 0 and g == 0):
                        act.wait_ge(recon_done, at(img, GROUPS * ND, g * ND))
                    act.activation(ct[:, :, t * P:(t + 1) * P], ct_ps[:], ACT.Copy).then_inc(ct_ready, 1)
                elif kind == "z":
                    t, = a
                    img, q = (i - 1, 1 - par) if t >= T else (i, par)
                    act.wait_ge(gn_step, at(img, 2 * GN_STEPS, 2 * GN_STEPS))
                    if not (isinstance(img, int) and img == 0 and t < 2):
                        act.wait_ge(corr_done, at(img, TILES, t - 1))
                    for ph in range(2):
                        rows = xa[q][:, 1 + t * TP + ph:1 + (t + 1) * TP:2, :]
                        last = act.activation(z[:, t % 2, ph].rearrange("p j (h w) -> p h w j", h=TP // 2),
                                              rows.rearrange("p h (w j) -> p h w j", j=PATCH), ACT.Identity,
                                              scale=fac[q][:, 1, 0:1], bias=fac[q][:, 1, 1:2])
                    last.then_inc(z_ready, 1)
                elif kind == "h":
                    t, = a
                    img = i - 1 if t >= T else i
                    act.wait_ge(corr_done, at(img, TILES, t + 1))
                    if not (isinstance(img, int) and img == 0):
                        act.wait_ge(picked, at(img, GROUPS * PICKS, (t // T + 1) * PICKS - GROUPS * PICKS))
                    act.activation(h[:, t, :], gen_ps[t % 2][:], ACT.Copy).then_inc(h_ready, 1)
                elif kind == "xn":
                    c, = a
                    if c == 0:
                        act.wait_ge(gn_step, at(i, 2 * GN_STEPS, GN_STEPS))
                        for n in range(2):
                            act.wait_ge(x_edge[n], at(i, 16, 16))
                    if not (isinstance(i, int) and i == 0 and c < XN_RING):
                        act.wait_ge(conv_done, at(i, CHUNKS, c - XN_RING + 1))
                    for tau in range(2):
                        src = 1 - tau
                        ps_, pd = slice(64 * src, 64 * src + 64), slice(64 * tau, 64 * tau + 64)
                        rows = slice(c * CP + tau, c * CP + tau + CP + 1)
                        sc, bi = fac[par][ps_, 0, 0:1], fac[par][ps_, 0, 1:2]
                        act.activation(xn[pd, c % XN_RING, :, 1:W + 1], xa[par][ps_, rows, :], ACT.Identity,
                                       scale=sc, bias=bi)
                        for to, of in ((0, W - 1), (W + 1, 0)):
                            last = act.activation(xn[pd, c % XN_RING, :, to:to + 1],
                                                  xa[par][ps_, rows, of:of + 1], ACT.Identity, scale=sc, bias=bi)
                    last.then_inc(xn_ready, 1)
                elif kind == "rt":
                    n, = a
                    act.wait_ge(gn_step, at(i, 2 * GN_STEPS, n * GN_STEPS + 5))
                    act.activation(gsc[:, 4:5], gsc[:, 3:4], ACT.Sqrt).then_inc(gn_root, 1)

            def period(i, par, loop=False):
                own, b, p = parts(i, loop)
                img = i - 1
                for s in range(SLOTS):
                    g, k, t = s // (KMAX * T), s // T % KMAX, s % T
                    if b:
                        if k > 0:
                            act.wait_ge(h_masked, at(img, LATER, (g * (KMAX - 1) + k - 1) * T + t + 1))
                        else:
                            act.wait_ge(h_ready, at(img, TILES, g * T + t + 1))
                        if not (isinstance(img, int) and img == 0 and s < 2):
                            act.wait_ge(atom_found, at(img, SLOTS, s - 1))
                        act.activation(score[s % 2][:], h[:, g * T + t, :], ACT.Abs).then_inc(score_ready, 1)
                    for what in SCALAR_PLAN.get(s, ()):
                        first = what[0] in OWN or (what[0] in "zh" and what[1] < T)
                        second = what[0] in "zh" and what[1] >= T or what[0] == "ct" and what[1] == 0
                        if own if first else b if second else p:
                            extra(what, i, par)

            periods(act, period)

        @block.vector
        def _(dve):
            def stop_until(sem_, value):
                dve.wait_ge(sem_, value)
                dve.sem_inc(vector_passed, 1)

            def extra(what, i, par):
                kind, *a = what
                if kind == "xs":
                    q, = a
                    dve.wait_ge(x_loaded[q], at(i, 16, 16))
                    for c in range(q * CHUNKS // QUARTERS, (q + 1) * CHUNKS // QUARTERS):
                        dve.bn_stats(bn[0][:, c, :], xa[par][:, 1 + c * CP:1 + (c + 1) * CP, :]).then_inc(x_stats, 1)
                elif kind == "ca":
                    c, = a
                    dve.wait_ge(conv_done, at(i, CHUNKS, c + 1))
                    dve.wait_ge(xn_ready, at(i, CHUNKS, min(c + 2, CHUNKS)))
                    dst = xa[par][:, 1 + c * CP:1 + (c + 1) * CP, :]
                    dve.tensor_tensor(dst, conv_ps[c % 2][:], dst, ALU.add).then_inc(x1_ready, 1)
                    if c > 0:
                        x1_stat(i, par, c - 1)
                elif kind == "zs":
                    x1_stat(i, par, CHUNKS - 1)
                elif kind == "gn":
                    gn_part(i, par, *a)
                elif kind == "ce":
                    g, t = a
                    img = i - 2 if g else i - 1
                    n = g * T + t
                    for j in range(KMAX):
                        if t == 0 and j == 0:
                            dve.wait_ge(alg_step, at(img, GROUPS * ALG, (g + 1) * ALG))
                        if not (isinstance(img, int) and img == 0 and n == 0):
                            dve.wait_ge(ce_turned, at(img, TILES * KMAX, (n - 1) * KMAX + j + 1))
                        dve.tensor_scalar(ce[:, j, :], count[:], which[:, g, j, t:t + 1], xc[:, g, j, t:t + 1],
                                          ALU.is_equal, ALU.mult).then_inc(ce_ready, 1)
                elif kind == "ra":
                    g, d = a
                    img, q = (i - 2, par) if g else (i - 1, 1 - par)
                    ph, pj = divmod(d, PATCH)
                    half = PAIRS // GROUPS
                    dst = xa[q][:, 1 + g * half + ph:1 + (g + 1) * half:2, :]\
                        .rearrange("p h (w j) -> p j h w", j=PATCH)[:, pj]
                    dve.wait_ge(recon_done, at(img, GROUPS * ND, g * ND + d + 1))
                    dve.tensor_tensor(dst, gen_ps[d % 2][:].rearrange("p (h w) -> p h w", h=half // 2), dst, ALU.add)\
                        .then_inc(recon_added, 1)

            def x1_stat(i, par, c):
                stop_until(x1_ready, at(i, CHUNKS, c + 1))
                dve.bn_stats(bn[1][:, c, :], xa[par][:, 1 + c * CP:1 + (c + 1) * CP, :]).then_inc(x1_stats, 1)

            def gn_part(i, par, n, part):
                base = n * GN_STEPS

                def after(step):
                    dve.wait_ge(gn_step, at(i, 2 * GN_STEPS, base + step))

                if part == 0:
                    stop_until(x1_stats if n else x_stats, at(i, CHUNKS, CHUNKS))
                    dve.bn_aggr(mv[:], bn[n][:].rearrange("p c s -> p (c s)")).then_inc(gn_step, 1)
                elif part == 1:
                    dve.wait_ge(gn_sum, at(i, 4, 2 * n + 1))
                    dve.tensor_copy(gsc[:, 0:1], st_ps[:, 0:1]).then_inc(gn_step, 1)
                    after(2)
                    dve.tensor_tensor(gsc[:, 1:2], mv[:, 0:1], gsc[:, 0:1], ALU.subtract).then_inc(gn_step, 1)
                    after(3)
                    dve.scalar_tensor_tensor(gsc[:, 2:3], gsc[:, 1:2], gsc[:, 1:2], mv[:, 1:2], ALU.mult, ALU.add)\
                        .then_inc(gn_step, 1)
                    dve.wait_ge(gn_sum, at(i, 4, 2 * n + 2))
                    dve.tensor_scalar(gsc[:, 3:4], st_ps[:, 1:2], GN_EPS, None, ALU.add).then_inc(gn_step, 1)
                else:
                    stop_until(gn_root, at(i, 2, n + 1))
                    dve.reciprocal(gsc[:, 5:6], gsc[:, 4:5]).then_inc(gn_step, 1)
                    after(6)
                    dve.tensor_tensor(gsc[:, 6:7], gsc[:, 3:4], gsc[:, 5:6], ALU.mult).then_inc(gn_step, 1)
                    after(7)
                    dve.tensor_scalar(gsc[:, 7:8], gsc[:, 6:7], gsc[:, 4:5], 0.5, ALU.add, ALU.mult)\
                        .then_inc(gn_step, 1)
                    after(8)
                    dve.reciprocal(fac[par][:, n, 0:1], gsc[:, 7:8]).then_inc(gn_step, 1)
                    after(9)
                    dve.tensor_scalar(fac[par][:, n, 1:2], gsc[:, 0:1], -1.0, fac[par][:, n, 0:1], ALU.mult, ALU.mult)\
                        .then_inc(gn_step, 1)

            def pursuit_step(img, g, k, between):
                base = (g * KMAX + k) * T
                later = (g * (KMAX - 1) + k - 1) * T
                picks = g * PICKS + T * sum(1 + j for j in range(k))

                def search(t):
                    n = base + t
                    stop_until(score_ready, at(img, SLOTS, n + 1))
                    dve.max(top8[:, t, :], score[n % 2][:]).then_inc(top_found, 1)

                def locate(t):
                    n = base + t
                    if k:
                        dve.wait_ge(row_loaded[t], at(img, 16 * GROUPS * (KMAX - 1), 16 * (g * (KMAX - 1) + k)))
                    stop_until(top_found, at(img, SLOTS, n + 1))
                    dve.max_index(idx8[:, t, :], top8[:, t, :], score[n % 2][:]).then_inc(atom_found, 1)

                def to_float(t):
                    dve.wait_ge(atom_found, at(img, SLOTS, base + t + 1))
                    dve.tensor_copy(which[:, g, k, t:t + 1], idx8[:, t, 0:1]).then_inc(which_ready, 1)

                def one_hot(t):
                    dve.wait_ge(which_ready, at(img, SLOTS, base + t + 1))
                    dve.tensor_scalar(hot[:, t, :], count[:], which[:, g, k, t:t + 1], None, ALU.is_equal)\
                        .then_inc(hot_ready, 1)
                    if k == 0:
                        dve.tensor_scalar(mask[:, t, :], count[:], which[:, g, k, t:t + 1], None, ALU.not_equal)\
                            .then_inc(mask_ready, 1)

                def pick(t):
                    n = picks + t * (k + 1)
                    dve.wait_ge(hot_ready, at(img, SLOTS, base + t + 1))
                    for j in range(-1, k):
                        if not (isinstance(img, int) and img == 0 and n < 4):
                            dve.wait_ge(picked, at(img, GROUPS * PICKS, n - 3))
                        dve.tensor_tensor_reduce(
                            out=junk[:, n % 4, :], in0=h[:, g * T + t, :] if j < 0 else u[:, t, j, :],
                            in1=hot[:, t, :], scale=1.0, scalar=0.0, op0=ALU.mult, op1=ALU.add,
                            accum_out=hsel[:, g, k, t:t + 1] if j < 0 else v[:, g, k, j, t:t + 1])\
                            .then_inc(picked, 1)
                        n += 1
                    if 0 < k < KMAX - 1:
                        dve.tensor_tensor(mask[:, t, :], mask[:, t, :], hot[:, t, :], ALU.subtract)\
                            .then_inc(mask_ready, 1)

                for t in range(T):
                    search(t)
                    if t > 0:
                        to_float(t - 1)
                    locate(t)
                    if t > 0:
                        one_hot(t - 1)
                        between(base + t - 1)
                        pick(t - 1)
                to_float(T - 1)
                one_hot(T - 1)
                between(base + T - 1)
                pick(T - 1)

            def algebra(img, g, k):
                n = g * ALG + (1 + 6 * (k - 1) - 1 if k > 1 else k)

                def after(step):
                    dve.wait_ge(alg_step, at(img, GROUPS * ALG, step))

                dve.wait_ge(picked, at(img, GROUPS * PICKS, g * PICKS + T * sum(1 + j for j in range(k + 1))))
                if k == 0:
                    dve.tensor_scalar(na[:, g, 0, :], hsel[:, g, 0, :], -1.0, None, ALU.mult).then_inc(alg_step, 1)
                    return
                after(n)
                dve.scalar_tensor_tensor(nl[:, g, k, 0:k, :], v[:, g, k, 0:k, :], -1.0, rd[:, g, 0:k, :],
                                         ALU.mult, ALU.mult).then_inc(alg_step, 1)
                after(n + 1)
                dst = sq[:, 0:k, :] if k > 1 else ss[:].rearrange("p (a t) -> p a t", a=1)
                dve.tensor_tensor(dst, nl[:, g, k, 0:k, :], v[:, g, k, 0:k, :], ALU.mult).then_inc(alg_step, 1)
                n += 2
                after(n)
                if k > 1:
                    dve.tensor_reduce(ss[:], sq[:, 0:k, :].rearrange("p j t -> p t j"), axis=AX.X, op=ALU.add)\
                        .then_inc(alg_step, 1)
                    n += 1
                    after(n)
                dve.tensor_scalar(dd[:], ss[:], 1.0, DIAG_EPS, ALU.add, ALU.max).then_inc(alg_step, 1)
                after(n + 1)
                dve.reciprocal(rd[:, g, k, :], dd[:]).then_inc(alg_step, 1)
                after(n + 2)
                dve.scalar_tensor_tensor(na[:, g, k, :], hsel[:, g, k, :], -1.0, rd[:, g, k, :], ALU.mult, ALU.mult)\
                    .then_inc(alg_step, 1)

            def coefficients(img, g):
                n = (g + 1) * ALG - 1 - 2 * (KMAX - 1)

                def after(step):
                    dve.wait_ge(alg_step, at(img, GROUPS * ALG, step))

                after(n)
                dve.tensor_scalar(xc[:, g], na[:, g], -1.0, None, ALU.mult).then_inc(alg_step, 1)
                n += 1
                for k in range(KMAX - 1, 0, -1):
                    after(n)
                    dve.tensor_tensor(tmp[:, 0:k, :], nl[:, g, k, 0:k, :],
                                      xc[:, g, k:k + 1, :].to_broadcast([P, k, T]), ALU.mult).then_inc(alg_step, 1)
                    after(n + 1)
                    dve.tensor_tensor(xc[:, g, 0:k, :], xc[:, g, 0:k, :], tmp[:, 0:k, :], ALU.add)\
                        .then_inc(alg_step, 1)
                    n += 2

            def project(img, g, k):
                rows = g * ROWS + T * sum(range(k))
                done = g * ALG + (1 if k == 0 else 6 * k)
                dve.wait_ge(alg_step, at(img, GROUPS * ALG, done))
                for j in range(k):
                    for t in range(T):
                        if j == 0:
                            dve.wait_ge(row_loaded[t], at(img, 16 * GROUPS * (KMAX - 1), 16 * (g * (KMAX - 1) + k + 1)))
                        else:
                            dve.wait_ge(row_step, at(img, GROUPS * ROWS, rows + (j - 1) * T + t + 1))
                        dve.scalar_tensor_tensor(u[:, t, k, :], u[:, t, j, :], nl[:, g, k, j, t:t + 1], u[:, t, k, :],
                                                 ALU.mult, ALU.add).then_inc(row_step, 1)
                for t in range(T):
                    if k == 0:
                        dve.wait_ge(row_loaded[t], at(img, 16 * GROUPS * (KMAX - 1), 16 * (g * (KMAX - 1) + 1)))
                    else:
                        dve.wait_ge(row_step, at(img, GROUPS * ROWS, rows + (k - 1) * T + t + 1))
                    hh = h[:, g * T + t, :]
                    dve.scalar_tensor_tensor(hh, u[:, t, k, :], na[:, g, k, t:t + 1], hh, ALU.mult, ALU.add)\
                        .then_inc(h_updated, 1)

            def period(i, par, loop=False):
                own, b, p = parts(i, loop)

                def between(s):
                    for what in VECTOR_PLAN.get(s, ()):
                        if own if what[0] in OWN else b if what[1] == 0 else p:
                            extra(what, i, par)

                for g in range(GROUPS):
                    for k in range(KMAX):
                        if not b:
                            for t in range(T):
                                between((g * KMAX + k) * T + t)
                            continue
                        pursuit_step(i - 1, g, k, between)
                        algebra(i - 1, g, k)
                        if k < KMAX - 1:
                            project(i - 1, g, k)
                    if b:
                        coefficients(i - 1, g)

            periods(dve, period)

        @block.tensor
        def _(pe):
            def turn(img, g):
                for t in range(T):
                    n = g * T + t
                    for j in range(KMAX):
                        pe.wait_ge(ce_ready, at(img, TILES * KMAX, n * KMAX + j + 1))
                        if j == 0 and not (isinstance(img, int) and img == 0 and n == 0):
                            pe.wait_ge(ct_ready, at(img, TILES, n))
                        for a in range(NA):
                            last = pe.matmul(ct_ps[:, a, :], ce[:, j, a * P:(a + 1) * P], ident[:], is_transpose=True,
                                             start=(j == 0 and a == 0), stop=(j == KMAX - 1), skip_group_check=True)
                        last.then_inc(ce_turned, 1)

            def recon(img, g):
                for d in range(ND):
                    if d == 0:
                        pe.wait_ge(ct_ready, at(img, TILES, (g + 1) * T))
                    if d < 2:
                        after = img + 1 if g else img
                        pe.wait_ge(h_ready, at(after, TILES, (T if g else TILES) - 1 + d)
                                   if not (isinstance(after, int) and after >= images) else at(images - 1, TILES, TILES))
                    else:
                        pe.wait_ge(recon_added, at(img, GROUPS * ND, g * ND + d - 1))
                    for a in range(NA):
                        last = pe.matmul(gen_ps[d % 2][:], dt_[:, a, d, :], ct[:, a, :], start=(a == 0), stop=(a == NA - 1))
                    last.then_inc(recon_done, 1)

            def correlate(img, half):
                for t in range(half * T, half * T + T):
                    pe.wait_ge(z_ready, at(img, TILES, t + 1))
                    if t % T >= 2:
                        pe.wait_ge(h_ready, at(img, TILES, t - 1))
                    elif not (isinstance(img, int) and img == 0):
                        pe.wait_ge(recon_added, at(img, GROUPS * ND, (1 + half) * ND - GROUPS * ND - 1 + t % T))
                    elif half:
                        pe.wait_ge(h_ready, t - 1)
                    for d in range(ND):
                        last = pe.matmul(gen_ps[t % 2][:], z[:, t % 2, d // PATCH, d % PATCH, :], dn[:, d, :],
                                         start=(d == 0), stop=(d == ND - 1))
                    last.then_inc(corr_done, 1)

            def average(i, n):
                pe.wait_ge(gn_step, at(i, 2 * GN_STEPS, n * GN_STEPS + 1))
                pe.matmul(st_ps[:, 0:1], avg[:], mv[:, 0:1], start=True, stop=True).then_inc(gn_sum, 1)
                pe.wait_ge(gn_step, at(i, 2 * GN_STEPS, n * GN_STEPS + 4))
                pe.matmul(st_ps[:, 1:2], avg[:], gsc[:, 2:3], start=True, stop=True).then_inc(gn_sum, 1)

            def convolve(i):
                for c in range(CHUNKS):
                    pe.wait_ge(xn_ready, at(i, CHUNKS, c + 1))
                    if not (isinstance(i, int) and i == 0 and c < 2):
                        pe.wait_ge(x1_ready, at(i, CHUNKS, c - 1))
                    for m in range(2 * TAPS):
                        rows, tap = divmod(m, TAPS)
                        last = pe.matmul(conv_ps[c % 2][:], wc[:, m, :], xn[:, c % XN_RING, rows:rows + CP, tap:tap + W],
                                         start=(m == 0), stop=(m == 2 * TAPS - 1))
                    last.then_inc(conv_done, 1)

            def period(i, par, loop=False):
                own, b, p = parts(i, loop)
                if p:
                    turn(i - 2, 1)
                    recon(i - 2, 1)
                if b:
                    correlate(i - 1, 1)
                if own:
                    average(i, 0)
                    convolve(i)
                if b:
                    turn(i - 1, 0)
                if own:
                    average(i, 1)
                if b:
                    recon(i - 1, 0)
                if own:
                    correlate(i, 0)

            periods(pe, period)


def setup(nc, ctx, sem, w_taps, atoms, ident_in, avg_in, gram, dn, dt_, wc, h, u, count, ident, avg,
          rd, gen_ps, ct_ps, st_ps):
    atoms_in = sem("atoms_in")
    consts_in = sem("consts_in")
    taps_in = sem("taps_in")
    cleared = sem("cleared")
    squared = sem("squared")
    summed = sem("summed")
    rooted = sem("rooted")
    inverse = sem("inverse")
    scaled = sem("scaled")
    gram_done = sem("gram_done")
    gram_copied = sem("gram_copied")
    gram_out = sem("gram_out")
    turned = sem("turned")
    turned_copied = sem("turned_copied")
    counted = sem("counted")
    ones = h[:, 7, 0:P]
    with nc.Block() as block:
        @block.sync
        def _(sp):
            sp.dma_start(dn[:], atoms).then_inc(atoms_in, 16)
            sp.dma_start(ident[:], ident_in).then_inc(consts_in, 16)
            sp.dma_start(avg[:], avg_in).then_inc(consts_in, 16)
            sp.wait_ge(cleared, 1)
            for row in range(2):
                for tau in range(2):
                    for s in range(2):
                        a = 2 * row + tau - s
                        if 0 <= a < TAPS:
                            sp.dma_start(wc[64 * tau:64 * tau + 64, row * TAPS:(row + 1) * TAPS, 64 * s:64 * s + 64],
                                         w_taps[:, a, :, :]).then_inc(taps_in, 16)
            sp.wait_ge(taps_in, 16 * 6)
            for a in range(NA):
                sp.wait_ge(gram_copied, 2 * a + 2)
                sp.dma_start(gram[a * P:(a + 1) * P, :], u[:, a, 0, :]).then_inc(gram_out, 16)
            sp.wait_ge(gram_out, 16 * NA)

        @block.gpsimd
        def _(pool):
            pool.iota(count[:], [[1, ATOMS]], base=0, channel_multiplier=0,
                      allow_small_or_imprecise_dtypes=True).then_inc(counted, 1)
            pool.wait_ge(counted, 1)

        @block.scalar
        def _(act):
            act.wait_ge(atoms_in, 16)
            for d in range(ND):
                act.activation(u[:, d // 2, d % 2, :], dn[:, d, :], ACT.Square).then_inc(squared, 1)
            act.wait_ge(summed, 1)
            act.activation(h[:, 0, :], st_ps[:], ACT.Sqrt).then_inc(rooted, 1)
            for n in range(2 * NA):
                act.wait_ge(turned, n + 1)
                a, half = divmod(n, 2)
                act.activation(dt_[:, a, half * 4:half * 4 + 4, :], ct_ps[:], ACT.Copy).then_inc(turned_copied, 1)

        @block.vector
        def _(dve):
            dve.memset(wc[:], 0.0).then_inc(cleared, 1)
            dve.memset(ones, 1.0).then_inc(cleared, 1)
            dve.memset(rd[:], 1.0)
            dve.wait_ge(rooted, 1)
            dve.tensor_scalar(h[:, 1, :], h[:, 0, :], 1e-20, None, ALU.max).then_inc(inverse, 1)
            dve.wait_ge(inverse, 1)
            dve.reciprocal(h[:, 2, :], h[:, 1, :]).then_inc(inverse, 1)
            dve.wait_ge(inverse, 2)
            dve.tensor_tensor(h[:, 3, :], st_ps[:], h[:, 2, :], ALU.mult).then_inc(inverse, 1)
            dve.wait_ge(inverse, 3)
            dve.tensor_tensor(h[:, 4, :], h[:, 3, :], h[:, 1, :], ALU.add).then_inc(inverse, 1)
            dve.wait_ge(inverse, 4)
            dve.tensor_scalar(h[:, 5, :], h[:, 4, :], 0.5, NORM_EPS, ALU.mult, ALU.add).then_inc(inverse, 1)
            dve.wait_ge(inverse, 5)
            dve.reciprocal(h[:, 6, :], h[:, 5, :]).then_inc(inverse, 1)
            dve.wait_ge(inverse, 6)
            for d in range(ND):
                dve.tensor_tensor(dn[:, d, :], dn[:, d, :], h[:, 6, :], ALU.mult).then_inc(scaled, 1)
            dve.wait_ge(consts_in, 32)
            for a in range(NA):
                dve.wait_ge(gram_done, a + 1)
                dve.tensor_copy(u[:, a, 0, :], gen_ps[a % 2][:]).then_inc(gram_copied, 1)
                dve.wait_ge(gram_copied, 2 * a + 1)
                diag = u[:, a, 0, a * P:(a + 1) * P]
                dve.scalar_tensor_tensor(diag, ident[:], DIAG_EPS, diag, ALU.mult, ALU.add).then_inc(gram_copied, 1)

        @block.tensor
        def _(pe):
            pe.wait_ge(cleared, 2)
            for d in range(ND):
                pe.wait_ge(squared, d + 1)
                last = pe.matmul(st_ps[:], ones, u[:, d // 2, d % 2, :], start=(d == 0), stop=(d == ND - 1))
            last.then_inc(summed, 1)
            pe.wait_ge(scaled, ND)
            for a in range(NA):
                if a >= 2:
                    pe.wait_ge(gram_copied, 2 * a - 3)
                for d in range(ND):
                    last = pe.matmul(gen_ps[a % 2][:], dn[:, d, a * P:(a + 1) * P], dn[:, d, :],
                                     start=(d == 0), stop=(d == ND - 1))
                last.then_inc(gram_done, 1)
            pe.wait_ge(consts_in, 32)
            for n in range(2 * NA):
                a, half = divmod(n, 2)
                if n >= 1:
                    pe.wait_ge(turned_copied, n)
                for m in range(4):
                    last = pe.transpose(ct_ps[:, m, :], dn[:, half * 4 + m, a * P:(a + 1) * P], ident[:])
                last.then_inc(turned, 1)


def kernel(x, L0_conv_weight, L1_conv_dictionary):
    import concourse.bacc as bacc
    from concourse.bass_utils import run_bass_kernel_spmd

    x, weight, dictionary = (np.asarray(a) for a in (x, L0_conv_weight, L1_conv_dictionary))
    images = x.shape[0]
    arrays = {
        "x_pairs": np.ascontiguousarray(x.reshape(images, CIN, PAIRS, 2, W).transpose(0, 3, 1, 2, 4))
                     .reshape(images, P, PAIRS, W),
        "w_taps": np.ascontiguousarray(weight.transpose(1, 2, 3, 0)),
        "atoms": np.ascontiguousarray(dictionary.reshape(CIN, 2, 2, PATCH, ATOMS).transpose(2, 0, 1, 3, 4))
                   .reshape(P, ND, ATOMS),
        "ident_in": np.eye(P, dtype=np.float32),
        "avg_in": np.kron(np.ones((2, 2)), np.kron(np.eye(CIN // 2), np.full((2, 2), 0.25))).astype(np.float32),
    }
    nc = bacc.Bacc("TRN2", target_bir_lowering=False, num_devices=1)
    ins = [nc.dram_tensor(n, a.shape, mybir.dt.from_np(a.dtype), kind="ExternalInput").ap() for n, a in arrays.items()]
    y = nc.dram_tensor("y_pairs", (images, P, PAIRS, W), F32, kind="ExternalOutput").ap()
    preact_conv_pursuit(nc, *ins, y)
    r = run_bass_kernel_spmd(nc, [arrays], core_ids=[0])
    got = r.results[0]["y_pairs"]
    return np.ascontiguousarray(got.reshape(images, 2, CIN, PAIRS, W).transpose(0, 2, 3, 1, 4)).reshape(x.shape)
```

```python
import numpy as np
import concourse.bass as bass
from concourse import mybir
from contextlib import ExitStack

F32 = mybir.dt.float32
F16 = mybir.dt.float16
BF16 = mybir.dt.bfloat16
U32 = mybir.dt.uint32
ALU = mybir.AluOpType
ACT = mybir.ActivationFunctionType
AX = mybir.AxisListType

P = 128
CIN = 64
W = 128
PAIRS = 64
TAPS = 3
PATCH = 4
DIM = CIN * PATCH * PATCH
ND = DIM // P
ATOMS = 512
NA = ATOMS // P
KMAX = 5
T = 4
GROUPS = 2
TILES = T * GROUPS
TP = PAIRS // TILES
CP = 4
CHUNKS = PAIRS // CP
SWEEP = 8
HALF = PAIRS // SWEEP // 2
SUMS = 4 * HALF + 4
QUARTERS = 4
QP = PAIRS // QUARTERS
XN_RING = 4
SLOTS = GROUPS * KMAX * T
GN_EPS = 1e-5
NORM_EPS = 1e-10
DIAG_EPS = 1e-5
GN_STEPS = 10
PICKS = T * (sum(1 + k for k in range(KMAX - 1)) + 1)
ROWS = T * sum(range(KMAX - 1))
ALG = 1 + 6 * (KMAX - 2) - 1
SOLVE = 6 + 1 + 2 * (KMAX - 1)

AHEAD = T + 2
TURN_AFTER = 13
AVERAGE_AFTER = 2

VECTOR_PLAN = {
    0: [("co", 1), ("ce", 1, 0), ("ce", 1, 1)], 1: [("ce", 1, 2), ("ce", 1, 3)],
    3.5: [("ra", 1, 0), ("ra", 1, 1), ("ra", 1, 2)], 4: [("ra", 1, 3)], 5: [("ra", 1, 4)], 6: [("ra", 1, 5)],
    7: [("ra", 1, 6)], 7.5: [("ra", 1, 7)], 10: [("gn", 0, 1), ("gn", 0, 2)], 11.5: [("ca", 0)],
    12: [("ca", 1)], 13: [("ca", 2), ("zs", 0), ("ca", 3), ("zs", 1)], 14: [("ca", 4), ("zs", 2), ("zs", 3)],
    15: [("zs", 4), ("ca", 5)], 15.5: [("ca", 6), ("zs", 5)], 16: [("ca", 7)], 17: [("zs", 6)],
    18: [("ca", 8), ("zs", 7)], 20: [("ca", 9), ("zs", 8), ("ca", 10), ("zs", 9)],
    21: [("co", 0), ("ce", 0, 0), ("ca", 11), ("ce", 0, 1), ("ce", 0, 2), ("ce", 0, 3), ("zs", 10), ("ca", 12)],
    23: [("zs", 11)], 23.5: [("ca", 13)], 25: [("zs", 12)],
    26: [("ca", 14), ("zs", 13), ("ca", 15), ("zs", 14), ("zs", 15), ("ra", 0, 0), ("gn", 1, 0)],
    27: [("ra", 0, 1), ("gn", 1, 1)], 27.5: [("gn", 1, 2), ("ra", 0, 2)], 28: [("ra", 0, 3)],
    29: [("ra", 0, 4)], 30: [("ra", 0, 5)], 31: [("ra", 0, 6)], 32: [("ra", 0, 7)],
}
POOL_PLAN = {
    16: [("vp", 0, 0), ("vp", 0, 1)], 19: [("vp", 0, 2)], 21: [("vp", 0, 3)],
    38: [("vp", 1, 0), ("vp", 1, 1), ("vp", 1, 2), ("vp", 1, 3)],
}
SCALAR_PLAN = {
    0: [("z", 6), ("h", 4), ("z", 7), ("h", 5)], 1: [("vs", 1, 2), ("vs", 1, 3)], 2: [("ct", 1, 0)],
    3: [("ct", 1, 1), ("ct", 1, 2), ("ct", 1, 3), ("st", 0)], 5: [("st", 1)], 6: [("st", 2)],
    7: [("st", 3), ("h", 6), ("h", 7)], 8: [("st", 4)], 9: [("st", 5)],
    11: [("st", 6), ("rt", 0), ("xn", 0), ("xn", 1), ("xn", 2), ("xn", 3)], 13: [("xn", 4)], 14: [("xn", 5)],
    15: [("xn", 6), ("xn", 7)], 16: [("xn", 8)], 18: [("xn", 9)], 20: [("vs", 0, 0), ("xn", 10)],
    21: [("vs", 0, 1), ("xn", 11), ("vs", 0, 2), ("xn", 12)], 22: [("vs", 0, 3)],
    23: [("ct", 0, 0), ("xn", 13), ("ct", 0, 1), ("ct", 0, 2), ("ct", 0, 3), ("xn", 14), ("xn", 15)],
    27: [("rt", 1)], 29: [("z", 0)], 30: [("z", 1)], 31: [("h", 0), ("z", 2)], 35: [("h", 1), ("z", 3)],
    36: [("h", 2), ("z", 4)], 38: [("h", 3), ("z", 5)], 39: [("vs", 1, 0), ("vs", 1, 1)],
}
OWN = ("st", "ca", "zs", "gn", "xn", "rt")


def lag(what, s):
    kind, n = what[0], what[-1]
    early = s < SLOTS // 2
    if kind in OWN:
        return 0
    if kind in "zh":
        return 0 if n < T else 1 if n >= AHEAD or early else 0
    return 2 if what[1] == 1 and early else 1


class Image:

    def __init__(self, turn, n):
        self.turn, self.n = turn, n

    def __sub__(self, less):
        return Image(self.turn, self.n - less)

    def __add__(self, more):
        return Image(self.turn, self.n + more)


def number(image):
    return image if isinstance(image, int) else image.turn * 2 + image.n


def at(image, per_image, n):
    if isinstance(image, int):
        return image * per_image + n
    return image.turn * (2 * per_image) + (image.n * per_image + n)


def preact_conv_pursuit(nc, x, w_taps, atoms, ident_in, avg_in, out):
    images = x.shape[0]
    gram = nc.dram_tensor("gram_rows", (ATOMS, ATOMS), F32).ap()

    ctx = ExitStack()
    with ctx:
        def sb(name, shape, dt=F32):
            return ctx.enter_context(nc.sbuf_tensor(name, shape, dt))

        def sem(name):
            return ctx.enter_context(nc.semaphore(name))

        xa = [sb(f"xa{n}", [P, PAIRS + 2, W]) for n in range(2)]
        xn = sb("xn", [P, XN_RING, CP + 1, W + 2])
        z = sb("z", [P, 2, 2, PATCH, P])
        dn = sb("dn", [P, ND, ATOMS])
        dt_ = sb("dt", [P, NA, ND, P])
        wc = sb("wc", [P, 2 * TAPS, P])
        h = sb("h", [P, TILES, ATOMS])
        u = sb("u", [P, T, KMAX - 1, ATOMS])
        hot = sb("hot", [P, T, ATOMS], BF16)
        mask = sb("mask", [P, T, ATOMS], F16)
        ce = sb("ce", [P, KMAX, ATOMS])
        ct = sb("ct", [P, NA, T * P])
        junk = sb("junk", [P, 4, ATOMS], BF16)
        count = sb("count", [P, ATOMS], F16)
        ident = sb("ident", [P, P])
        avg = sb("avg", [P, P])
        top8 = sb("top8", [P, T, 8])
        idx8 = sb("idx8", [P, T, 8], U32)
        which = sb("which", [P, GROUPS, KMAX, T])
        hsel = sb("hsel", [P, GROUPS, KMAX, T])
        v = sb("v", [P, GROUPS, KMAX, KMAX, T])
        rd = sb("rd", [P, GROUPS, KMAX, T])
        nl = sb("nl", [P, GROUPS, KMAX, KMAX, T])
        na = sb("na", [P, GROUPS, KMAX, T])
        sq = sb("sq", [P, KMAX, T])
        ss = sb("ss", [P, T])
        dd = sb("dd", [P, T])
        xc = sb("xc", [P, GROUPS, KMAX, T])
        sq_last = sb("sq_last", [P, KMAX - 1, T])
        ss_last = sb("ss_last", [P, T])
        dd_last = sb("dd_last", [P, T])
        tmp = sb("tmp", [P, KMAX, T])
        bn = sb("bn", [P, CHUNKS, 6])
        mv = sb("mv", [P, 2, 2])
        minus_shift = sb("minus_shift", [P, 1])
        shifted = sb("shifted", [P, 2])
        sums = sb("sums", [P, 2, PAIRS // SWEEP])
        junk_sums = sb("junk_sums", [P, SWEEP, W], BF16)
        gsc = sb("gsc", [P, 8])
        fac = [sb(f"fac{n}", [P, 2, 2]) for n in range(2)]

        conv_ps = [ctx.enter_context(nc.psum_tensor(f"conv_ps{n}", [P, CP, W], F32)) for n in range(2)]
        gen_ps = [ctx.enter_context(nc.psum_tensor(f"gen_ps{n}", [P, ATOMS], F32)) for n in range(2)]
        ct_ps = ctx.enter_context(nc.psum_tensor("ct_ps", [P, NA, P], F32))
        score = [ctx.enter_context(nc.psum_tensor(f"score{n}", [P, ATOMS], F32)) for n in range(2)]
        st_ps = ctx.enter_context(nc.psum_tensor("st_ps", [P, ATOMS], F32))

        x_loaded = [sem(f"x_loaded{q}") for q in range(QUARTERS)]
        x_edge = [sem(f"x_edge{n}") for n in range(2)]
        vector_passed = sem("vector_passed")
        pool_passed = sem("pool_passed")
        sync_passed = sem("sync_passed")
        out_stored = [sem(f"out_stored{q}") for q in range(QUARTERS)]
        x_sums = sem("x_sums")
        gn_step = sem("gn_step")
        gn_sum = sem("gn_sum")
        gn_root = sem("gn_root")
        xn_ready = sem("xn_ready")
        conv_done = sem("conv_done")
        x1_ready = sem("x1_ready")
        x1_stats = sem("x1_stats")
        z_ready = sem("z_ready")
        corr_done = sem("corr_done")
        h_ready = sem("h_ready")
        h_updated = sem("h_updated")
        h_masked = sem("h_masked")
        score_ready = sem("score_ready")
        top_found = sem("top_found")
        atom_found = sem("atom_found")
        which_ready = sem("which_ready")
        hot_ready = sem("hot_ready")
        mask_ready = sem("mask_ready")
        picked = sem("picked")
        alg_step = sem("alg_step")
        v_product = sem("v_product")
        v_summed = sem("v_summed")
        solve_step = sem("solve_step")
        row_step = sem("row_step")
        row_loaded = [sem(f"row_loaded{t}") for t in range(T)]
        ce_ready = sem("ce_ready")
        ce_turned = sem("ce_turned")
        ct_ready = sem("ct_ready")
        recon_done = sem("recon_done")
        recon_added = sem("recon_added")

        LATER = SLOTS - GROUPS * T

        def loaded(eng, q, image, par):
            eng.dma_start(xa[par][:, 1 + q * QP:1 + (q + 1) * QP, :], x[number(image)][:, q * QP:(q + 1) * QP, :])\
                .then_inc(x_loaded[q], 16)
            if q == 0:
                eng.dma_start(xa[par][:, PAIRS + 1, :], x[number(image)][:, 0, :]).then_inc(x_edge[0], 16)
            if q == QUARTERS - 1:
                eng.dma_start(xa[par][:, 0, :], x[number(image)][:, PAIRS - 1, :]).then_inc(x_edge[1], 16)

        def x_statistics(act, i, par, part):

            def step(m, out_, in_, func, accum, done=x_sums, **args):
                if m or not (isinstance(i, int) and i == 0):
                    act.wait_ge(x_sums, at(i, SUMS, m))
                act.activation(out_, in_, func, accum_out=accum, **args).then_inc(done, 1)

            def total(n, square):
                rows = xa[par][:, 1 + n * SWEEP:1 + (n + 1) * SWEEP, :]
                m = n + square * (HALF + 1) if n < HALF else 2 * n + 1 + square
                if square:
                    step(m, junk_sums[:], rows, ACT.Square, sums[:, 1, n:n + 1], bias=minus_shift[:, 0:1])
                else:
                    step(m, junk_sums[:], rows, ACT.Identity, sums[:, 0, n:n + 1])

            few = junk_sums[:, 0, 0:2 * HALF]
            mean_ = 1.0 / (PAIRS * W)
            if part < 6:
                q = part % 2 if part < 4 else part - 2
                if part < 2 or part >= 4:
                    act.wait_ge(x_loaded[q], at(i, 16, 16))
                for n in (2 * q, 2 * q + 1):
                    if part < 2 or part >= 4:
                        total(n, 0)
                    if part >= 2:
                        total(n, 1)
                if part == 1:
                    step(HALF, few[:, 0:HALF], sums[:, 0, 0:HALF], ACT.Identity, minus_shift[:, 0:1],
                         scale=-2 * mean_)
            else:
                step(4 * HALF + 1, few, sums[:, 0, :], ACT.Identity, mv[:, 0, 0:1], scale=mean_)
                step(4 * HALF + 2, few, sums[:, 1, :], ACT.Identity, shifted[:, 0:1], scale=mean_)
                step(4 * HALF + 3, few[:, 0:1], mv[:, 0, 0:1], ACT.Square, shifted[:, 1:2],
                     bias=minus_shift[:, 0:1])
                act.wait_ge(x_sums, at(i, SUMS, 4 * HALF + 4))
                act.activation(mv[:, 0, 1:2], shifted[:, 1:2], ACT.Identity, scale=-1.0,
                               bias=shifted[:, 0:1]).then_inc(gn_step, 1)

        def periods(eng, period):
            period(0, 0)
            period(1, 1)
            with eng.Fori(0, (images - 2) // 2) as j:
                period(Image(j, 2), 0, True)
                period(Image(j, 3), 1, True)
            period(images, 0)
            period(images + 1, 1)

        def parts(i, loop):
            if loop:
                return True, True, True
            return i < images, 1 <= i <= images, i >= 2

        def first_loads(sp):
            for q in range(QUARTERS):
                loaded(sp, q, 0, 0)

        def first_statistics(act):
            for part in range(7):
                x_statistics(act, 0, 0, part)

        setup(nc, ctx, sem, w_taps, atoms, ident_in, avg_in, gram, dn, dt_, wc, h, u, count, ident, avg,
              rd, gen_ps, ct_ps, st_ps, first_loads, first_statistics)

        block = ctx.enter_context(nc.Block())

        @block.sync
        def _(sp):
            sp.wait_ge(x_edge[0], 16)
            for q in range(QUARTERS // 2):
                sp.wait_ge(x_loaded[q], 16)
                loaded(sp, q, 1, 1)

            def stop_until(sem_, value):
                sp.wait_ge(sem_, value)
                sp.sem_inc(sync_passed, 1)

            def period(i, par, loop=False):
                own, b, p = parts(i, loop)
                if p:
                    stop_until(recon_added, at(i, 2 * ND, -2 * ND))
                    for q in (2, 3):
                        sp.dma_start(out[number(i - 2)][:, q * QP:(q + 1) * QP, :], xa[par][:, 1 + q * QP:1 + (q + 1) * QP, :])\
                            .then_inc(out_stored[q], 16)
                if own:
                    for q in (2, 3):
                        if p:
                            stop_until(out_stored[q], at(i, 16, -16))
                        elif i == 1:
                            stop_until(x_loaded[q], 16)
                            if q == QUARTERS - 1:
                                stop_until(x_edge[1], 16)
                        if not (isinstance(i, int) and i == 0):
                            loaded(sp, q, i, par)
                if b:
                    stop_until(recon_added, at(i, 2 * ND, -ND))
                    for q in (0, 1):
                        sp.dma_start(out[number(i - 1)][:, q * QP:(q + 1) * QP, :],
                                     xa[1 - par][:, 1 + q * QP:1 + (q + 1) * QP, :]).then_inc(out_stored[q], 16)
                    if loop or i + 1 < images:
                        for q in (0, 1):
                            stop_until(out_stored[q], at(i, 16, 0))
                            loaded(sp, q, i + 1, 1 - par)

            period(0, 0)
            period(1, 1)
            with sp.Fori(0, (images - 4) // 2) as j:
                period(Image(j, 2), 0, True)
                period(Image(j, 3), 1, True)
            for i in range(images - 2, images + 2):
                period(i, i % 2)
            for q in range(QUARTERS):
                sp.wait_ge(out_stored[q], 16 * images)

        @block.gpsimd
        def _(pool):
            def stop_until(sem_, value):
                pool.wait_ge(sem_, value)
                pool.sem_inc(pool_passed, 1)

            def extra(what, i, par, back):
                kind, *a = what
                if kind == "vp":
                    g, t = a
                    pool.wait_ge(hot_ready, at(i - back, SLOTS, (g * KMAX + KMAX - 1) * T + t + 1))
                    for j in range(KMAX - 1):
                        pool.tensor_tensor(u[:, t, j, :], u[:, t, j, :], hot[:, t, :], ALU.mult).then_inc(v_product, 1)

            def period(i, par, loop=False):
                here = own, b, p = parts(i, loop)
                img = i - 1
                for g in range(GROUPS):
                    for k in range(KMAX):
                        for t in range(T if b and k > 0 else 0):
                            n = (g * (KMAX - 1) + k - 1) * T + t
                            pool.wait_ge(h_updated, at(img, LATER, n + 1))
                            pool.tensor_tensor(h[:, g * T + t, :], h[:, g * T + t, :], mask[:, t, :], ALU.mult)\
                                .then_inc(h_masked, 1)
                        for t in range(T):
                            n = (g * KMAX + k) * T + t
                            if b and k < KMAX - 1:
                                stop_until(atom_found, at(img, SLOTS, n + 1))
                                if k == 0 and not (isinstance(img, int) and img == 0 and g == 0):
                                    stop_until(v_summed, at(img, TILES * (KMAX - 1), (g * T + t + 1 - T) * (KMAX - 1)))
                                pool.indirect_dma_start(u[:, t, k, :], None, gram,
                                                        bass.IndirectOffsetOnAxis(ap=idx8[:, t, 0:1], axis=0))\
                                    .then_inc(row_loaded[t], 16)
                            for what in POOL_PLAN.get(n, ()):
                                if here[lag(what, n)]:
                                    extra(what, i, par, lag(what, n))

            periods(pool, period)

        @block.scalar
        def _(act):
            def extra(what, i, par, back):
                kind, *a = what
                if kind == "ct":
                    g, t = a
                    img = i - back
                    n = g * T + t
                    act.wait_ge(ce_turned, at(img, TILES * KMAX, (n + 1) * KMAX))
                    if not (isinstance(img, int) and img == 0 and g == 0):
                        act.wait_ge(recon_done, at(img, GROUPS * ND, g * ND))
                    act.activation(ct[:, :, t * P:(t + 1) * P], ct_ps[:], ACT.Copy).then_inc(ct_ready, 1)
                elif kind == "vs":
                    g, t = a
                    for j in range(KMAX - 1):
                        act.wait_ge(v_product, at(i - back, TILES * (KMAX - 1), (g * T + t) * (KMAX - 1) + j + 1))
                        act.activation(u[:, t, j, :], u[:, t, j, :], ACT.Copy,
                                       accum_out=v[:, g, KMAX - 1, j, t:t + 1]).then_inc(v_summed, 1)
                elif kind == "z":
                    t, = a
                    img, q = i - back, 1 - par if back else par
                    act.wait_ge(gn_step, at(img, 2 * GN_STEPS, 2 * GN_STEPS))
                    if not (isinstance(img, int) and img == 0 and t < 2):
                        act.wait_ge(corr_done, at(img, TILES, t - 1))
                    for ph in range(2):
                        rows = xa[q][:, 1 + t * TP + ph:1 + (t + 1) * TP:2, :]
                        last = act.activation(z[:, t % 2, ph].rearrange("p j (h w) -> p h w j", h=TP // 2),
                                              rows.rearrange("p h (w j) -> p h w j", j=PATCH), ACT.Identity,
                                              scale=fac[q][:, 1, 0:1], bias=fac[q][:, 1, 1:2])
                    last.then_inc(z_ready, 1)
                elif kind == "h":
                    t, = a
                    img = i - back
                    act.wait_ge(corr_done, at(img, TILES, t + 1))
                    if not (isinstance(img, int) and img == 0):
                        act.wait_ge(picked, at(img, GROUPS * PICKS, (t // T + 1) * PICKS - T + t % T + 1 - GROUPS * PICKS))
                    act.activation(h[:, t, :], gen_ps[t % 2][:], ACT.Copy).then_inc(h_ready, 1)
                elif kind == "xn":
                    c, = a
                    if c == 0:
                        act.wait_ge(gn_step, at(i, 2 * GN_STEPS, GN_STEPS))
                        for n in range(2):
                            act.wait_ge(x_edge[n], at(i, 16, 16))
                    if not (isinstance(i, int) and i == 0 and c < XN_RING):
                        act.wait_ge(conv_done, at(i, CHUNKS, c - XN_RING + 1))
                    for tau in range(2):
                        src = 1 - tau
                        ps_, pd = slice(64 * src, 64 * src + 64), slice(64 * tau, 64 * tau + 64)
                        rows = slice(c * CP + tau, c * CP + tau + CP + 1)
                        sc, bi = fac[par][ps_, 0, 0:1], fac[par][ps_, 0, 1:2]
                        act.activation(xn[pd, c % XN_RING, :, 1:W + 1], xa[par][ps_, rows, :], ACT.Identity,
                                       scale=sc, bias=bi)
                        for to, of in ((0, W - 1), (W + 1, 0)):
                            last = act.activation(xn[pd, c % XN_RING, :, to:to + 1],
                                                  xa[par][ps_, rows, of:of + 1], ACT.Identity, scale=sc, bias=bi)
                    last.then_inc(xn_ready, 1)
                elif kind == "st":
                    if not (isinstance(i, int) and i == 0):
                        x_statistics(act, i, par, *a)
                elif kind == "rt":
                    n, = a
                    act.wait_ge(gn_step, at(i, 2 * GN_STEPS, n * GN_STEPS + 5))
                    act.activation(gsc[:, 4:5], gsc[:, 3:4], ACT.Sqrt).then_inc(gn_root, 1)

            def period(i, par, loop=False):
                here = own, b, p = parts(i, loop)
                img = i - 1
                for s in range(SLOTS):
                    g, k, t = s // (KMAX * T), s // T % KMAX, s % T
                    if b:
                        if k > 0:
                            act.wait_ge(h_masked, at(img, LATER, (g * (KMAX - 1) + k - 1) * T + t + 1))
                        else:
                            act.wait_ge(h_ready, at(img, TILES, g * T + t + 1))
                        if not (isinstance(img, int) and img == 0 and s < 2):
                            act.wait_ge(atom_found, at(img, SLOTS, s - 1))
                        act.activation(score[s % 2][:], h[:, g * T + t, :], ACT.Abs).then_inc(score_ready, 1)
                    for what in SCALAR_PLAN.get(s, ()):
                        if here[lag(what, s)]:
                            extra(what, i, par, lag(what, s))

            periods(act, period)

        @block.vector
        def _(dve):
            def stop_until(sem_, value):
                dve.wait_ge(sem_, value)
                dve.sem_inc(vector_passed, 1)

            def extra(what, i, par, back):
                kind, *a = what
                if kind == "ca":
                    c, = a
                    dve.wait_ge(conv_done, at(i, CHUNKS, c + 1))
                    dve.wait_ge(xn_ready, at(i, CHUNKS, min(c + 2, CHUNKS)))
                    dst = xa[par][:, 1 + c * CP:1 + (c + 1) * CP, :]
                    dve.tensor_tensor(dst, conv_ps[c % 2][:], dst, ALU.add).then_inc(x1_ready, 1)
                elif kind == "ra":
                    g, d = a
                    img, q = i - back, par if back == 2 else 1 - par
                    ph, pj = divmod(d, PATCH)
                    half = PAIRS // GROUPS
                    dst = xa[q][:, 1 + g * half + ph:1 + (g + 1) * half:2, :]\
                        .rearrange("p h (w j) -> p j h w", j=PATCH)[:, pj]
                    dve.wait_ge(recon_done, at(img, GROUPS * ND, g * ND + d + 1))
                    dve.tensor_tensor(dst, gen_ps[d % 2][:].rearrange("p (h w) -> p h w", h=half // 2), dst, ALU.add)\
                        .then_inc(recon_added, 1)
                elif kind == "zs":
                    x1_stat(i, par, *a)
                elif kind == "gn":
                    gn_part(i, par, *a)
                elif kind == "co":
                    coefficients(i - back, *a)
                elif kind == "ce":
                    g, t = a
                    img = i - back
                    n = g * T + t
                    for j in range(KMAX):
                        if t == 0 and j == 0:
                            dve.wait_ge(which_ready, at(img, GROUPS * KMAX, (g + 1) * KMAX))
                            dve.wait_ge(solve_step, at(img, GROUPS * SOLVE, (g + 1) * SOLVE))
                        if not (isinstance(img, int) and img == 0 and n == 0):
                            dve.wait_ge(ce_turned, at(img, TILES * KMAX, (n - 1) * KMAX + j + 1))
                        dve.tensor_scalar(ce[:, j, :], count[:], which[:, g, j, t:t + 1], xc[:, g, j, t:t + 1],
                                          ALU.is_equal, ALU.mult).then_inc(ce_ready, 1)

            def x1_stat(i, par, c):
                stop_until(x1_ready, at(i, CHUNKS, c + 1))
                dve.bn_stats(bn[:, c, :], xa[par][:, 1 + c * CP:1 + (c + 1) * CP, :]).then_inc(x1_stats, 1)

            def gn_part(i, par, n, part):
                base = n * GN_STEPS

                def after(step):
                    dve.wait_ge(gn_step, at(i, 2 * GN_STEPS, base + step))

                if part == 0:
                    stop_until(x1_stats, at(i, CHUNKS, CHUNKS))
                    dve.bn_aggr(mv[:, 1, :], bn[:].rearrange("p c s -> p (c s)")).then_inc(gn_step, 1)
                elif part == 1:
                    dve.wait_ge(gn_sum, at(i, 4, 2 * n + 1))
                    dve.tensor_copy(gsc[:, 0:1], st_ps[:, 0:1]).then_inc(gn_step, 1)
                    after(2)
                    dve.tensor_tensor(gsc[:, 1:2], mv[:, n, 0:1], gsc[:, 0:1], ALU.subtract).then_inc(gn_step, 1)
                    after(3)
                    dve.scalar_tensor_tensor(gsc[:, 2:3], gsc[:, 1:2], gsc[:, 1:2], mv[:, n, 1:2], ALU.mult, ALU.add)\
                        .then_inc(gn_step, 1)
                    dve.wait_ge(gn_sum, at(i, 4, 2 * n + 2))
                    dve.tensor_scalar(gsc[:, 3:4], st_ps[:, 1:2], GN_EPS, None, ALU.add).then_inc(gn_step, 1)
                else:
                    stop_until(gn_root, at(i, 2, n + 1))
                    dve.reciprocal(gsc[:, 5:6], gsc[:, 4:5]).then_inc(gn_step, 1)
                    after(6)
                    dve.tensor_tensor(gsc[:, 6:7], gsc[:, 3:4], gsc[:, 5:6], ALU.mult).then_inc(gn_step, 1)
                    after(7)
                    dve.tensor_scalar(gsc[:, 7:8], gsc[:, 6:7], gsc[:, 4:5], 0.5, ALU.add, ALU.mult)\
                        .then_inc(gn_step, 1)
                    after(8)
                    dve.reciprocal(fac[par][:, n, 0:1], gsc[:, 7:8]).then_inc(gn_step, 1)
                    after(9)
                    dve.tensor_scalar(fac[par][:, n, 1:2], gsc[:, 0:1], -1.0, fac[par][:, n, 0:1], ALU.mult, ALU.mult)\
                        .then_inc(gn_step, 1)

            def pursuit_step(img, g, k, between):
                base = (g * KMAX + k) * T
                later = (g * (KMAX - 1) + k - 1) * T
                picks = g * PICKS + T * sum(1 + j for j in range(k))

                def search(t):
                    n = base + t
                    stop_until(score_ready, at(img, SLOTS, n + 1))
                    dve.max(top8[:, t, :], score[n % 2][:]).then_inc(top_found, 1)

                def locate(t):
                    n = base + t
                    if k:
                        dve.wait_ge(row_loaded[t], at(img, 16 * GROUPS * (KMAX - 1), 16 * (g * (KMAX - 1) + k)))
                    stop_until(top_found, at(img, SLOTS, n + 1))
                    dve.max_index(idx8[:, t, :], top8[:, t, :], score[n % 2][:]).then_inc(atom_found, 1)

                def one_hot(t):
                    dve.wait_ge(atom_found, at(img, SLOTS, base + t + 1))
                    if k == 0 and not (isinstance(img, int) and img == 0 and g == 0):
                        dve.wait_ge(v_product, at(img, TILES * (KMAX - 1), (g * T + t + 1 - T) * (KMAX - 1)))
                    dve.tensor_scalar(hot[:, t, :], count[:], idx8[:, t, 0:1], None, ALU.is_equal)\
                        .then_inc(hot_ready, 1)
                    if k == 0:
                        dve.tensor_scalar(mask[:, t, :], count[:], idx8[:, t, 0:1], None, ALU.not_equal)\
                            .then_inc(mask_ready, 1)

                def pick(t):
                    count_here = k + 1 if k < KMAX - 1 else 1
                    n = picks + t * count_here
                    dve.wait_ge(hot_ready, at(img, SLOTS, base + t + 1))
                    for j in range(-1, count_here - 1):
                        if not (isinstance(img, int) and img == 0 and n < 4):
                            dve.wait_ge(picked, at(img, GROUPS * PICKS, n - 3))
                        dve.tensor_tensor_reduce(
                            out=junk[:, n % 4, :], in0=h[:, g * T + t, :] if j < 0 else u[:, t, j, :],
                            in1=hot[:, t, :], scale=1.0, scalar=0.0, op0=ALU.mult, op1=ALU.add,
                            accum_out=hsel[:, g, k, t:t + 1] if j < 0 else v[:, g, k, j, t:t + 1])\
                            .then_inc(picked, 1)
                        n += 1
                    if 0 < k < KMAX - 1:
                        dve.tensor_tensor(mask[:, t, :], mask[:, t, :], hot[:, t, :], ALU.subtract)\
                            .then_inc(mask_ready, 1)

                for t in range(T):
                    search(t)
                    if t > 0:
                        one_hot(t - 1)
                    locate(t)
                    if t > 0:
                        between(base + t - 1)
                        pick(t - 1)
                one_hot(T - 1)
                dve.tensor_copy(which[:, g, k, :], idx8[:, :, 0]).then_inc(which_ready, 1)
                between(base + T - 1)
                pick(T - 1)

            def factor_row(g, k, wait, step, n, squares, total, pivot):
                wait(n)
                dve.scalar_tensor_tensor(nl[:, g, k, 0:k, :], v[:, g, k, 0:k, :], -1.0, rd[:, g, 0:k, :],
                                         ALU.mult, ALU.mult).then_inc(step, 1)
                wait(n + 1)
                dst = squares[:, 0:k, :] if k > 1 else total[:].rearrange("p (a t) -> p a t", a=1)
                dve.tensor_tensor(dst, nl[:, g, k, 0:k, :], v[:, g, k, 0:k, :], ALU.mult).then_inc(step, 1)
                n += 2
                wait(n)
                if k > 1:
                    dve.tensor_reduce(total[:], squares[:, 0:k, :].rearrange("p j t -> p t j"), axis=AX.X, op=ALU.add)\
                        .then_inc(step, 1)
                    n += 1
                    wait(n)
                dve.tensor_scalar(pivot[:], total[:], 1.0, DIAG_EPS, ALU.add, ALU.max).then_inc(step, 1)
                wait(n + 1)
                dve.reciprocal(rd[:, g, k, :], pivot[:]).then_inc(step, 1)
                wait(n + 2)
                dve.scalar_tensor_tensor(na[:, g, k, :], hsel[:, g, k, :], -1.0, rd[:, g, k, :], ALU.mult, ALU.mult)\
                    .then_inc(step, 1)

            def algebra(img, g, k):
                dve.wait_ge(picked, at(img, GROUPS * PICKS, g * PICKS + T * sum(1 + j for j in range(k + 1))))
                if k == 0:
                    dve.tensor_scalar(na[:, g, 0, :], hsel[:, g, 0, :], -1.0, None, ALU.mult).then_inc(alg_step, 1)
                    return

                def wait(n):
                    dve.wait_ge(alg_step, at(img, GROUPS * ALG, n))

                factor_row(g, k, wait, alg_step, g * ALG + (1 + 6 * (k - 1) - 1 if k > 1 else 1), sq, ss, dd)

            def coefficients(img, g):
                n = g * SOLVE

                def wait(n):
                    dve.wait_ge(solve_step, at(img, GROUPS * SOLVE, n))

                dve.wait_ge(alg_step, at(img, GROUPS * ALG, (g + 1) * ALG))
                dve.wait_ge(picked, at(img, GROUPS * PICKS, (g + 1) * PICKS))
                stop_until(v_summed, at(img, TILES * (KMAX - 1), (g + 1) * T * (KMAX - 1)))
                factor_row(g, KMAX - 1, wait if g else lambda n: wait(n) if n else None, solve_step, n,
                           sq_last, ss_last, dd_last)
                n += 6
                wait(n)
                dve.tensor_scalar(xc[:, g], na[:, g], -1.0, None, ALU.mult).then_inc(solve_step, 1)
                n += 1
                for k in range(KMAX - 1, 0, -1):
                    wait(n)
                    dve.tensor_tensor(tmp[:, 0:k, :], nl[:, g, k, 0:k, :],
                                      xc[:, g, k:k + 1, :].to_broadcast([P, k, T]), ALU.mult).then_inc(solve_step, 1)
                    wait(n + 1)
                    dve.tensor_tensor(xc[:, g, 0:k, :], xc[:, g, 0:k, :], tmp[:, 0:k, :], ALU.add)\
                        .then_inc(solve_step, 1)
                    n += 2

            def project(img, g, k, between):
                rows = g * ROWS + T * sum(range(k))
                done = g * ALG + (1 if k == 0 else 6 * k)
                dve.wait_ge(alg_step, at(img, GROUPS * ALG, done))
                for pair in range(0, T, 2):
                    row = rows + pair * k
                    for j in range(k):
                        for t in (pair, pair + 1):
                            if j == 0:
                                dve.wait_ge(row_loaded[t],
                                            at(img, 16 * GROUPS * (KMAX - 1), 16 * (g * (KMAX - 1) + k + 1)))
                            else:
                                dve.wait_ge(row_step, at(img, GROUPS * ROWS, row + (j - 1) * 2 + t - pair + 1))
                            dve.scalar_tensor_tensor(u[:, t, k, :], u[:, t, j, :], nl[:, g, k, j, t:t + 1],
                                                     u[:, t, k, :], ALU.mult, ALU.add).then_inc(row_step, 1)
                    for t in (pair, pair + 1):
                        if k == 0:
                            dve.wait_ge(row_loaded[t], at(img, 16 * GROUPS * (KMAX - 1), 16 * (g * (KMAX - 1) + 1)))
                        else:
                            dve.wait_ge(row_step, at(img, GROUPS * ROWS, row + (k - 1) * 2 + t - pair + 1))
                        hh = h[:, g * T + t, :]
                        dve.scalar_tensor_tensor(hh, u[:, t, k, :], na[:, g, k, t:t + 1], hh, ALU.mult, ALU.add)\
                            .then_inc(h_updated, 1)
                    if pair == 0:
                        between((g * KMAX + k + 1) * T - 0.5)

            def period(i, par, loop=False):
                here = own, b, p = parts(i, loop)

                def between(s):
                    for what in VECTOR_PLAN.get(s, ()):
                        if here[lag(what, s)]:
                            extra(what, i, par, lag(what, s))

                for g in range(GROUPS):
                    for k in range(KMAX):
                        if not b:
                            for t in range(T):
                                between((g * KMAX + k) * T + t)
                            if k < KMAX - 1:
                                between((g * KMAX + k + 1) * T - 0.5)
                            continue
                        pursuit_step(i - 1, g, k, between)
                        if k < KMAX - 1:
                            algebra(i - 1, g, k)
                            project(i - 1, g, k, between)

            periods(dve, period)

        @block.tensor
        def _(pe):
            def turn(img, g):
                for t in range(T):
                    n = g * T + t
                    for j in range(KMAX):
                        pe.wait_ge(ce_ready, at(img, TILES * KMAX, n * KMAX + j + 1))
                        if j == 0 and not (isinstance(img, int) and img == 0 and n == 0):
                            pe.wait_ge(ct_ready, at(img, TILES, n))
                        for a in range(NA):
                            last = pe.matmul(ct_ps[:, a, :], ce[:, j, a * P:(a + 1) * P], ident[:], is_transpose=True,
                                             start=(j == 0 and a == 0), stop=(j == KMAX - 1), skip_group_check=True)
                        last.then_inc(ce_turned, 1)

            def recon(img, g, between=lambda done: None):
                for d in range(ND):
                    if d == 0:
                        pe.wait_ge(ct_ready, at(img, TILES, (g + 1) * T))
                    if d < 2:
                        after = img + 1 if g else img
                        pe.wait_ge(h_ready, at(after, TILES, (AHEAD if g else TILES) - 1 + d)
                                   if not (isinstance(after, int) and after >= images) else at(images - 1, TILES, TILES))
                    else:
                        pe.wait_ge(recon_added, at(img, GROUPS * ND, g * ND + d - 1))
                    for a in range(NA):
                        last = pe.matmul(gen_ps[d % 2][:], dt_[:, a, d, :], ct[:, a, :], start=(a == 0), stop=(a == NA - 1))
                    last.then_inc(recon_done, 1)
                    between(d + 1)

            def correlate(img, tiles):
                for t in tiles:
                    pe.wait_ge(z_ready, at(img, TILES, t + 1))
                    first = isinstance(img, int) and img == 0
                    if t < 2 and not first:
                        pe.wait_ge(recon_added, at(img, GROUPS * ND, t - 1 - ND))
                    elif t >= AHEAD and not first:
                        pe.wait_ge(recon_added, at(img, GROUPS * ND, t - AHEAD - 1))
                    elif t >= 2:
                        pe.wait_ge(h_ready, at(img, TILES, t - 1))
                    for d in range(ND):
                        last = pe.matmul(gen_ps[t % 2][:], z[:, t % 2, d // PATCH, d % PATCH, :], dn[:, d, :],
                                         start=(d == 0), stop=(d == ND - 1))
                    last.then_inc(corr_done, 1)

            def average(i, n):
                pe.wait_ge(gn_step, at(i, 2 * GN_STEPS, n * GN_STEPS + 1))
                pe.matmul(st_ps[:, 0:1], avg[:], mv[:, n, 0:1], start=True, stop=True).then_inc(gn_sum, 1)
                pe.wait_ge(gn_step, at(i, 2 * GN_STEPS, n * GN_STEPS + 4))
                pe.matmul(st_ps[:, 1:2], avg[:], gsc[:, 2:3], start=True, stop=True).then_inc(gn_sum, 1)

            def convolve(i, between):
                for c in range(CHUNKS):
                    pe.wait_ge(xn_ready, at(i, CHUNKS, c + 1))
                    if not (isinstance(i, int) and i == 0 and c < 2):
                        pe.wait_ge(x1_ready, at(i, CHUNKS, c - 1))
                    for m in range(2 * TAPS):
                        rows, tap = divmod(m, TAPS)
                        last = pe.matmul(conv_ps[c % 2][:], wc[:, m, :], xn[:, c % XN_RING, rows:rows + CP, tap:tap + W],
                                         start=(m == 0), stop=(m == 2 * TAPS - 1))
                    last.then_inc(conv_done, 1)
                    between(c + 1)

            def period(i, par, loop=False):
                own, b, p = parts(i, loop)
                if p:
                    turn(i - 2, 1)
                    recon(i - 2, 1)
                if b:
                    correlate(i - 1, range(AHEAD, TILES))
                if own:
                    average(i, 0)
                    convolve(i, lambda done: turn(i - 1, 0) if b and done == TURN_AFTER else None)
                elif b:
                    turn(i - 1, 0)
                if b:
                    recon(i - 1, 0, lambda done: average(i, 1) if own and done == AVERAGE_AFTER else None)
                elif own:
                    average(i, 1)
                if own:
                    correlate(i, range(AHEAD))

            periods(pe, period)


def setup(nc, ctx, sem, w_taps, atoms, ident_in, avg_in, gram, dn, dt_, wc, h, u, count, ident, avg,
          rd, gen_ps, ct_ps, st_ps, first_loads, first_statistics):
    atoms_in = sem("atoms_in")
    consts_in = sem("consts_in")
    taps_in = sem("taps_in")
    cleared = sem("cleared")
    squared = sem("squared")
    summed = sem("summed")
    rooted = sem("rooted")
    inverse = sem("inverse")
    scaled = sem("scaled")
    gram_done = sem("gram_done")
    gram_copied = sem("gram_copied")
    gram_out = sem("gram_out")
    turned = sem("turned")
    turned_copied = sem("turned_copied")
    counted = sem("counted")
    ones = h[:, 7, 0:P]
    with nc.Block() as block:
        @block.sync
        def _(sp):
            sp.dma_start(dn[:], atoms).then_inc(atoms_in, 16)
            sp.dma_start(ident[:], ident_in).then_inc(consts_in, 16)
            sp.dma_start(avg[:], avg_in).then_inc(consts_in, 16)
            sp.wait_ge(cleared, 1)
            for row in range(2):
                for tau in range(2):
                    for s in range(2):
                        a = 2 * row + tau - s
                        if 0 <= a < TAPS:
                            sp.dma_start(wc[64 * tau:64 * tau + 64, row * TAPS:(row + 1) * TAPS, 64 * s:64 * s + 64],
                                         w_taps[:, a, :, :]).then_inc(taps_in, 16)
            first_loads(sp)
            sp.wait_ge(taps_in, 16 * 6)
            for a in range(NA):
                sp.wait_ge(gram_copied, 2 * a + 2)
                sp.dma_start(gram[a * P:(a + 1) * P, :], u[:, a, 0, :]).then_inc(gram_out, 16)
            sp.wait_ge(gram_out, 16 * NA)

        @block.gpsimd
        def _(pool):
            pool.iota(count[:], [[1, ATOMS]], base=0, channel_multiplier=0,
                      allow_small_or_imprecise_dtypes=True).then_inc(counted, 1)
            pool.wait_ge(counted, 1)

        @block.scalar
        def _(act):
            act.wait_ge(atoms_in, 16)
            for d in range(ND):
                act.activation(u[:, d // 2, d % 2, :], dn[:, d, :], ACT.Square).then_inc(squared, 1)
            act.wait_ge(summed, 1)
            act.activation(h[:, 0, :], st_ps[:], ACT.Sqrt).then_inc(rooted, 1)
            first_statistics(act)
            for n in range(2 * NA):
                act.wait_ge(turned, n + 1)
                a, half = divmod(n, 2)
                act.activation(dt_[:, a, half * 4:half * 4 + 4, :], ct_ps[:], ACT.Copy).then_inc(turned_copied, 1)

        @block.vector
        def _(dve):
            dve.memset(wc[:], 0.0).then_inc(cleared, 1)
            dve.memset(ones, 1.0).then_inc(cleared, 1)
            dve.memset(rd[:], 1.0)
            dve.wait_ge(rooted, 1)
            dve.tensor_scalar(h[:, 1, :], h[:, 0, :], 1e-20, None, ALU.max).then_inc(inverse, 1)
            dve.wait_ge(inverse, 1)
            dve.reciprocal(h[:, 2, :], h[:, 1, :]).then_inc(inverse, 1)
            dve.wait_ge(inverse, 2)
            dve.tensor_tensor(h[:, 3, :], st_ps[:], h[:, 2, :], ALU.mult).then_inc(inverse, 1)
            dve.wait_ge(inverse, 3)
            dve.tensor_tensor(h[:, 4, :], h[:, 3, :], h[:, 1, :], ALU.add).then_inc(inverse, 1)
            dve.wait_ge(inverse, 4)
            dve.tensor_scalar(h[:, 5, :], h[:, 4, :], 0.5, NORM_EPS, ALU.mult, ALU.add).then_inc(inverse, 1)
            dve.wait_ge(inverse, 5)
            dve.reciprocal(h[:, 6, :], h[:, 5, :]).then_inc(inverse, 1)
            dve.wait_ge(inverse, 6)
            for d in range(ND):
                dve.tensor_tensor(dn[:, d, :], dn[:, d, :], h[:, 6, :], ALU.mult).then_inc(scaled, 1)
            dve.wait_ge(consts_in, 32)
            for a in range(NA):
                dve.wait_ge(gram_done, a + 1)
                dve.tensor_copy(u[:, a, 0, :], gen_ps[a % 2][:]).then_inc(gram_copied, 1)
                dve.wait_ge(gram_copied, 2 * a + 1)
                diag = u[:, a, 0, a * P:(a + 1) * P]
                dve.scalar_tensor_tensor(diag, ident[:], DIAG_EPS, diag, ALU.mult, ALU.add).then_inc(gram_copied, 1)

        @block.tensor
        def _(pe):
            pe.wait_ge(cleared, 2)
            for d in range(ND):
                pe.wait_ge(squared, d + 1)
                last = pe.matmul(st_ps[:], ones, u[:, d // 2, d % 2, :], start=(d == 0), stop=(d == ND - 1))
            last.then_inc(summed, 1)
            pe.wait_ge(scaled, ND)
            for a in range(NA):
                if a >= 2:
                    pe.wait_ge(gram_copied, 2 * a - 3)
                for d in range(ND):
                    last = pe.matmul(gen_ps[a % 2][:], dn[:, d, a * P:(a + 1) * P], dn[:, d, :],
                                     start=(d == 0), stop=(d == ND - 1))
                last.then_inc(gram_done, 1)
            pe.wait_ge(consts_in, 32)
            for n in range(2 * NA):
                a, half = divmod(n, 2)
                if n >= 1:
                    pe.wait_ge(turned_copied, n)
                for m in range(4):
                    last = pe.transpose(ct_ps[:, m, :], dn[:, half * 4 + m, a * P:(a + 1) * P], ident[:])
                last.then_inc(turned, 1)


def kernel(x, L0_conv_weight, L1_conv_dictionary):
    import concourse.bacc as bacc
    from concourse.bass_utils import run_bass_kernel_spmd

    x, weight, dictionary = (np.asarray(a) for a in (x, L0_conv_weight, L1_conv_dictionary))
    images = x.shape[0]
    arrays = {
        "x_pairs": np.ascontiguousarray(x.reshape(images, CIN, PAIRS, 2, W).transpose(0, 3, 1, 2, 4))
                     .reshape(images, P, PAIRS, W),
        "w_taps": np.ascontiguousarray(weight.transpose(1, 2, 3, 0)),
        "atoms": np.ascontiguousarray(dictionary.reshape(CIN, 2, 2, PATCH, ATOMS).transpose(2, 0, 1, 3, 4))
                   .reshape(P, ND, ATOMS),
        "ident_in": np.eye(P, dtype=np.float32),
        "avg_in": np.kron(np.ones((2, 2)), np.kron(np.eye(CIN // 2), np.full((2, 2), 0.25))).astype(np.float32),
    }
    nc = bacc.Bacc("TRN2", target_bir_lowering=False, num_devices=1)
    ins = [nc.dram_tensor(n, a.shape, mybir.dt.from_np(a.dtype), kind="ExternalInput").ap() for n, a in arrays.items()]
    y = nc.dram_tensor("y_pairs", (images, P, PAIRS, W), F32, kind="ExternalOutput").ap()
    preact_conv_pursuit(nc, *ins, y)
    r = run_bass_kernel_spmd(nc, [arrays], core_ids=[0])
    got = r.results[0]["y_pairs"]
    return np.ascontiguousarray(got.reshape(images, 2, CIN, PAIRS, W).transpose(0, 2, 3, 1, 4)).reshape(x.shape)
```

```python
import numpy as np
import concourse.bass as bass
from concourse import mybir
from contextlib import ExitStack

F32 = mybir.dt.float32
F16 = mybir.dt.float16
BF16 = mybir.dt.bfloat16
U32 = mybir.dt.uint32
ALU = mybir.AluOpType
ACT = mybir.ActivationFunctionType
AX = mybir.AxisListType

P = 128
CIN = 64
W = 128
PAIRS = 64
TAPS = 3
PATCH = 4
DIM = CIN * PATCH * PATCH
ND = DIM // P
ATOMS = 512
NA = ATOMS // P
KMAX = 5
T = 4
GROUPS = 2
TILES = T * GROUPS
TP = PAIRS // TILES
CP = 4
CHUNKS = PAIRS // CP
SWEEP = 8
HALF = PAIRS // SWEEP // 2
SUMS = 4 * HALF + 4
PARTS = 5 + HALF
TWO = 2
QUARTERS = 4
QP = PAIRS // QUARTERS
XN_RING = 4
SLOTS = GROUPS * KMAX * T
GN_EPS = 1e-5
NORM_EPS = 1e-10
DIAG_EPS = 1e-5
GN_STEPS = 10
ROWS = T * sum(range(KMAX - 1))
ALG = 1 + 6 * (KMAX - 2) - 1
SOLVE = 6 + 1 + 2 * (KMAX - 1)

AHEAD = T + 2
TURN_AFTER = 13
AVERAGE_AFTER = 3

VECTOR_PLAN = {
    0: [("co", 1), ("ce", 1, 0), ("ce", 1, 1), ("ce", 1, 2), ("ce", 1, 3)], 1: [("ra", 1, 0)],
    3: [("ra", 1, 1)], 3.5: [("ra", 1, 2)], 4: [("ra", 1, 3)], 5: [("ra", 1, 4), ("ra", 1, 5)],
    6: [("ra", 1, 6)], 7: [("ra", 1, 7)], 9: [("gn", 0, 1)], 10: [("gn", 0, 2)], 11.5: [("ca", 0)],
    12: [("ca", 1)], 13: [("ca", 2), ("ca", 3)], 14: [("ca", 4)], 15.5: [("ca", 5), ("ca", 6)], 16: [("ca", 7)],
    18: [("ca", 8), ("ca", 9)], 20: [("ca", 10), ("co", 0), ("ce", 0, 0)],
    21: [("ce", 0, 1), ("ca", 11), ("ce", 0, 2), ("ca", 12), ("ce", 0, 3)], 23.5: [("ca", 13)],
    24: [("ca", 14)], 25: [("ca", 15)], 27: [("ra", 0, 0)], 27.5: [("gn", 1, 1), ("ra", 0, 1)],
    28: [("ra", 0, 2), ("gn", 1, 2), ("ra", 0, 3)], 30: [("ra", 0, 4)], 31: [("ra", 0, 5)],
    31.5: [("ra", 0, 6)], 32: [("ra", 0, 7)],
}
POOL_PLAN = {
    16: [("vp", 0, 0)], 18: [("vp", 0, 1)], 38: [("vp", 1, 0)],
}
SCALAR_PLAN = {
    2: [("z", 6), ("h", 4)],
    3: [("h", 5), ("ct", 1, 0), ("z", 7), ("ct", 1, 1), ("ct", 1, 2), ("ct", 1, 3), ("st", 0)], 6: [("st", 1)],
    7: [("st", 2), ("st", 3), ("st", 4), ("h", 6), ("st", 5)], 9: [("st", 6), ("st", 7)], 10: [("st", 8)],
    11: [("h", 7), ("rt", 0), ("xn", 0), ("xn", 1), ("xn", 2), ("xn", 3)], 13: [("xn", 4)], 14: [("xn", 5)],
    15: [("xn", 6), ("xn", 7), ("xn", 8), ("st", 9)], 17: [("xn", 9)], 18: [("st", 10)],
    19: [("vs", 0, 0), ("xn", 10), ("vs", 0, 1)], 20: [("st", 11), ("xn", 11)], 21: [("st", 12), ("xn", 12)],
    22: [("st", 13)],
    23: [("ct", 0, 0), ("xn", 13), ("ct", 0, 1), ("st", 14), ("ct", 0, 2), ("ct", 0, 3), ("xn", 14), ("xn", 15)],
    25: [("st", 15)], 27: [("st", 16), ("st", 17), ("rt", 1)], 29: [("z", 0)], 34: [("z", 1), ("h", 0)],
    35: [("z", 2)], 36: [("h", 1), ("z", 3), ("h", 2)], 37: [("z", 4)], 39: [("z", 5), ("vs", 1, 0), ("h", 3)],
}
AWAY = [(0, 0), (0, 1), (1, 0)]
OWN = ("st", "ca", "gn", "xn", "rt")


def lag(what, s):
    kind, n = what[0], what[-1]
    early = s < SLOTS // 2
    if kind in OWN:
        return 0
    if kind in "zh":
        return 0 if n < T else 1 if n >= AHEAD or early else 0
    return 2 if what[1] == 1 and early else 1


def picks(g, k, t):
    return 1 + (k if k < KMAX - 1 or (g, t) not in AWAY else 0)


def picks_before(g, k, t=0):
    steps = [(a, b, c) for a in range(GROUPS) for b in range(KMAX) for c in range(T)]
    return sum(picks(*step) for step in steps if step < (g, k, t))


def away_before(g, t=0):
    return (KMAX - 1) * sum(tile < (g, t) for tile in AWAY)


PICKS = picks_before(GROUPS, 0)
PICKS_AWAY = away_before(GROUPS)


class Image:

    def __init__(self, turn, n):
        self.turn, self.n = turn, n

    def __sub__(self, less):
        return Image(self.turn, self.n - less)

    def __add__(self, more):
        return Image(self.turn, self.n + more)


def number(image):
    return image if isinstance(image, int) else image.turn * 2 + image.n


def at(image, per_image, n):
    if isinstance(image, int):
        return image * per_image + n
    return image.turn * (2 * per_image) + (image.n * per_image + n)


def preact_conv_pursuit(nc, x, w_taps, atoms, ident_in, avg_in, out):
    images = x.shape[0]
    gram = nc.dram_tensor("gram_rows", (ATOMS, ATOMS), F32).ap()

    ctx = ExitStack()
    with ctx:
        def sb(name, shape, dt=F32):
            return ctx.enter_context(nc.sbuf_tensor(name, shape, dt))

        def sem(name):
            return ctx.enter_context(nc.semaphore(name))

        xa = [sb(f"xa{n}", [P, PAIRS + 2, W]) for n in range(2)]
        xn = sb("xn", [P, XN_RING, CP + 1, W + 2])
        z = sb("z", [P, 2, 2, PATCH, P])
        dn = sb("dn", [P, ND, ATOMS])
        dt_ = sb("dt", [P, NA, ND, P])
        wc = sb("wc", [P, 2 * TAPS, P])
        h = sb("h", [P, TILES, ATOMS])
        u = sb("u", [P, T, KMAX - 1, ATOMS])
        hot = sb("hot", [P, T, ATOMS], BF16)
        mask = sb("mask", [P, T, ATOMS], F16)
        ce = sb("ce", [P, KMAX, ATOMS])
        ct = sb("ct", [P, NA, T * P])
        junk = sb("junk", [P, 4, ATOMS], BF16)
        count = sb("count", [P, ATOMS], F16)
        ident = sb("ident", [P, P])
        avg = sb("avg", [P, P])
        top8 = sb("top8", [P, T, 8])
        idx8 = sb("idx8", [P, T, 8], U32)
        which = sb("which", [P, GROUPS, KMAX, T])
        hsel = sb("hsel", [P, GROUPS, KMAX, T])
        v = sb("v", [P, GROUPS, KMAX, KMAX, T])
        rd = sb("rd", [P, GROUPS, KMAX, T])
        nl = sb("nl", [P, GROUPS, KMAX, KMAX, T])
        na = sb("na", [P, GROUPS, KMAX, T])
        sq = sb("sq", [P, KMAX, T])
        ss = sb("ss", [P, T])
        dd = sb("dd", [P, T])
        xc = sb("xc", [P, GROUPS, KMAX, T])
        sq_last = sb("sq_last", [P, KMAX - 1, T])
        ss_last = sb("ss_last", [P, T])
        dd_last = sb("dd_last", [P, T])
        tmp = sb("tmp", [P, KMAX, T])
        mv = sb("mv", [P, 2, 2])
        minus_shift = sb("minus_shift", [P, 1])
        shifted = sb("shifted", [P, 2])
        sums = sb("sums", [P, 2, PAIRS // SWEEP])
        junk_sums = sb("junk_sums", [P, SWEEP, W], BF16)
        gsc = sb("gsc", [P, 8])
        fac = [sb(f"fac{n}", [P, 2, 2]) for n in range(2)]

        conv_ps = [ctx.enter_context(nc.psum_tensor(f"conv_ps{n}", [P, CP, W], F32)) for n in range(2)]
        gen_ps = [ctx.enter_context(nc.psum_tensor(f"gen_ps{n}", [P, ATOMS], F32)) for n in range(2)]
        ct_ps = ctx.enter_context(nc.psum_tensor("ct_ps", [P, NA, P], F32))
        score = [ctx.enter_context(nc.psum_tensor(f"score{n}", [P, ATOMS], F32)) for n in range(2)]
        st_ps = ctx.enter_context(nc.psum_tensor("st_ps", [P, ATOMS], F32))

        x_loaded = [sem(f"x_loaded{q}") for q in range(QUARTERS)]
        x_edge = [sem(f"x_edge{n}") for n in range(2)]
        vector_passed = sem("vector_passed")
        pool_passed = sem("pool_passed")
        sync_passed = sem("sync_passed")
        out_stored = [sem(f"out_stored{q}") for q in range(QUARTERS)]
        x_sums = sem("x_sums")
        gn_step = sem("gn_step")
        gn_sum = sem("gn_sum")
        gn_root = sem("gn_root")
        xn_ready = sem("xn_ready")
        conv_done = sem("conv_done")
        x1_ready = sem("x1_ready")
        z_ready = sem("z_ready")
        corr_done = sem("corr_done")
        h_ready = sem("h_ready")
        h_updated = sem("h_updated")
        h_masked = sem("h_masked")
        score_ready = sem("score_ready")
        top_found = sem("top_found")
        atom_found = sem("atom_found")
        which_ready = sem("which_ready")
        hot_ready = sem("hot_ready")
        mask_ready = sem("mask_ready")
        picked = sem("picked")
        alg_step = sem("alg_step")
        v_product = sem("v_product")
        v_summed = sem("v_summed")
        solve_step = sem("solve_step")
        row_step = sem("row_step")
        row_loaded = [sem(f"row_loaded{t}") for t in range(T)]
        ce_ready = sem("ce_ready")
        ce_turned = sem("ce_turned")
        ct_ready = sem("ct_ready")
        recon_done = sem("recon_done")
        recon_added = sem("recon_added")

        LATER = SLOTS - GROUPS * T

        def quarter(q, first=0):
            if q < 2:
                return slice(first + q * QP, first + (q + 1) * QP)
            return slice(first + PAIRS // 2 + q - 2, first + PAIRS, 2)

        def loaded(eng, q, image, par):
            eng.dma_start(xa[par][:, quarter(q, 1), :], x[number(image)][:, quarter(q), :]).then_inc(x_loaded[q], 16)
            if q == 0:
                eng.dma_start(xa[par][:, PAIRS + 1, :], x[number(image)][:, 0, :]).then_inc(x_edge[0], 16)
            if q == QUARTERS - 1:
                eng.dma_start(xa[par][:, 0, :], x[number(image)][:, PAIRS - 1, :]).then_inc(x_edge[1], 16)

        def statistics(act, i, par, part):
            n, part = divmod(part, PARTS)

            def step(m, out_, in_, func, accum, **args):
                if n or m or not (isinstance(i, int) and i == 0):
                    act.wait_ge(x_sums, at(i, 2 * TWO * SUMS, TWO * (n * SUMS + m)))
                act.activation(out_, in_, func, accum_out=accum, **args).then_inc(x_sums, TWO)

            def total(c, square):
                if not square:
                    if n:
                        act.wait_ge(x1_ready, at(i, CHUNKS, (c + 1) * SWEEP // CP))
                    elif c * SWEEP % QP == 0:
                        act.wait_ge(x_loaded[c * SWEEP // QP], at(i, 16, 16))
                rows = xa[par][:, 1 + c * SWEEP:1 + (c + 1) * SWEEP, :]
                if n == 0 and c >= HALF:
                    q, part_of = 2 + (c - HALF) * SWEEP // QP, (c - HALF) * SWEEP % QP
                    rows = xa[par][:, quarter(q, 1), :][:, part_of:part_of + SWEEP, :]
                m = c + square * (HALF + 1) if c < HALF else 2 * c + 1 + square
                if square:
                    step(m, junk_sums[:], rows, ACT.Square, sums[:, 1, c:c + 1], bias=minus_shift[:, 0:1])
                else:
                    step(m, junk_sums[:], rows, ACT.Identity, sums[:, 0, c:c + 1])

            few = junk_sums[:, 0, 0:2 * HALF]
            one_of = 1.0 / (PAIRS * W)
            if part < 4:
                for c in range(part % 2 * HALF // 2, (part % 2 + 1) * HALF // 2):
                    total(c, part // 2)
                if part == 1:
                    step(HALF, few[:, 0:HALF], sums[:, 0, 0:HALF], ACT.Identity, minus_shift[:, 0:1],
                         scale=-2 * one_of)
            elif part < PARTS - 1:
                total(part - 4 + HALF, 0)
                total(part - 4 + HALF, 1)
            else:
                step(4 * HALF + 1, few, sums[:, 0, :], ACT.Identity, mv[:, n, 0:1], scale=one_of)
                step(4 * HALF + 2, few, sums[:, 1, :], ACT.Identity, shifted[:, 0:1], scale=one_of)
                step(4 * HALF + 3, few[:, 0:1], mv[:, n, 0:1], ACT.Square, shifted[:, 1:2],
                     bias=minus_shift[:, 0:1])
                act.wait_ge(x_sums, at(i, 2 * TWO * SUMS, TWO * (n + 1) * SUMS))
                act.activation(mv[:, n, 1:2], shifted[:, 1:2], ACT.Identity, scale=-1.0,
                               bias=shifted[:, 0:1]).then_inc(gn_step, 1)

        def periods(eng, period):
            period(0, 0)
            period(1, 1)
            with eng.Fori(0, (images - 2) // 2) as j:
                period(Image(j, 2), 0, True)
                period(Image(j, 3), 1, True)
            period(images, 0)
            period(images + 1, 1)

        def parts(i, loop):
            if loop:
                return True, True, True
            return i < images, 1 <= i <= images, i >= 2

        def first_loads(sp):
            for q in range(QUARTERS):
                loaded(sp, q, 0, 0)

        def first_statistics(act):
            for part in range(PARTS):
                statistics(act, 0, 0, part)

        setup(nc, ctx, sem, w_taps, atoms, ident_in, avg_in, gram, dn, dt_, wc, h, u, count, ident, avg,
              rd, gen_ps, ct_ps, st_ps, first_loads, first_statistics)

        block = ctx.enter_context(nc.Block())

        @block.sync
        def _(sp):
            sp.wait_ge(x_edge[0], 16)
            for q in range(QUARTERS // 2):
                sp.wait_ge(x_loaded[q], 16)
                loaded(sp, q, 1, 1)

            def stop_until(sem_, value):
                sp.wait_ge(sem_, value)
                sp.sem_inc(sync_passed, 1)

            def period(i, par, loop=False):
                own, b, p = parts(i, loop)
                for q in (2, 3):
                    if p:
                        stop_until(recon_added, at(i, 2 * ND, (q - 3) * ND // 2 - 2 * ND))
                        sp.dma_start(out[number(i - 2)][:, quarter(q), :], xa[par][:, quarter(q, 1), :])\
                            .then_inc(out_stored[q], 16)
                    if own:
                        if p:
                            stop_until(out_stored[q], at(i, 16, -16))
                        elif i == 1:
                            stop_until(x_loaded[q], 16)
                            if q == QUARTERS - 1:
                                stop_until(x_edge[1], 16)
                        if not (isinstance(i, int) and i == 0):
                            loaded(sp, q, i, par)
                if b:
                    stop_until(recon_added, at(i, 2 * ND, -ND))
                    for q in (0, 1):
                        sp.dma_start(out[number(i - 1)][:, quarter(q), :], xa[1 - par][:, quarter(q, 1), :])\
                            .then_inc(out_stored[q], 16)
                    if loop or i + 1 < images:
                        for q in (0, 1):
                            stop_until(out_stored[q], at(i, 16, 0))
                            loaded(sp, q, i + 1, 1 - par)

            period(0, 0)
            period(1, 1)
            with sp.Fori(0, (images - 4) // 2) as j:
                period(Image(j, 2), 0, True)
                period(Image(j, 3), 1, True)
            for i in range(images - 2, images + 2):
                period(i, i % 2)
            for q in range(QUARTERS):
                sp.wait_ge(out_stored[q], 16 * images)

        @block.gpsimd
        def _(pool):
            def stop_until(sem_, value):
                pool.wait_ge(sem_, value)
                pool.sem_inc(pool_passed, 1)

            def extra(what, i, par, back):
                kind, *a = what
                if kind == "vp":
                    g, t = a
                    pool.wait_ge(hot_ready, at(i - back, SLOTS, (g * KMAX + KMAX - 1) * T + t + 1))
                    for j in range(KMAX - 1):
                        pool.tensor_tensor(u[:, t, j, :], u[:, t, j, :], hot[:, t, :], ALU.mult).then_inc(v_product, 1)

            def period(i, par, loop=False):
                here = own, b, p = parts(i, loop)
                img = i - 1
                for g in range(GROUPS):
                    for k in range(KMAX):
                        for t in range(T if b and k > 0 else 0):
                            n = (g * (KMAX - 1) + k - 1) * T + t
                            pool.wait_ge(h_updated, at(img, LATER, n + 1))
                            pool.tensor_tensor(h[:, g * T + t, :], h[:, g * T + t, :], mask[:, t, :], ALU.mult)\
                                .then_inc(h_masked, 1)
                        for t in range(T):
                            n = (g * KMAX + k) * T + t
                            if b and k < KMAX - 1:
                                stop_until(atom_found, at(img, SLOTS, n + 1))
                                if k == 0 and not (isinstance(img, int) and img == 0 and g == 0) \
                                        and (1 - g, t) in AWAY:
                                    stop_until(v_summed, at(img, PICKS_AWAY, away_before(1 - g, t) + KMAX - 1
                                                            - (0 if g else PICKS_AWAY)))
                                pool.indirect_dma_start(u[:, t, k, :], None, gram,
                                                        bass.IndirectOffsetOnAxis(ap=idx8[:, t, 0:1], axis=0))\
                                    .then_inc(row_loaded[t], 16)
                            for what in POOL_PLAN.get(n, ()):
                                if here[lag(what, n)]:
                                    extra(what, i, par, lag(what, n))

            periods(pool, period)

        @block.scalar
        def _(act):
            def extra(what, i, par, back):
                kind, *a = what
                if kind == "ct":
                    g, t = a
                    img = i - back
                    n = g * T + t
                    act.wait_ge(ce_turned, at(img, TILES * KMAX, (n + 1) * KMAX))
                    if not (isinstance(img, int) and img == 0 and g == 0):
                        act.wait_ge(recon_done, at(img, GROUPS * ND, g * ND))
                    act.activation(ct[:, :, t * P:(t + 1) * P], ct_ps[:], ACT.Copy).then_inc(ct_ready, 1)
                elif kind == "vs":
                    g, t = a
                    for j in range(KMAX - 1):
                        act.wait_ge(v_product, at(i - back, PICKS_AWAY, away_before(g, t) + j + 1))
                        act.activation(u[:, t, j, :], u[:, t, j, :], ACT.Copy,
                                       accum_out=v[:, g, KMAX - 1, j, t:t + 1]).then_inc(v_summed, 1)
                elif kind == "z":
                    t, = a
                    img, q = i - back, 1 - par if back else par
                    act.wait_ge(gn_step, at(img, 2 * GN_STEPS, 2 * GN_STEPS))
                    if not (isinstance(img, int) and img == 0 and t < 2):
                        act.wait_ge(corr_done, at(img, TILES, t - 1))
                    for ph in range(2):
                        rows = xa[q][:, 1 + t * TP + ph:1 + (t + 1) * TP:2, :]
                        last = act.activation(z[:, t % 2, ph].rearrange("p j (h w) -> p h w j", h=TP // 2),
                                              rows.rearrange("p h (w j) -> p h w j", j=PATCH), ACT.Identity,
                                              scale=fac[q][:, 1, 0:1], bias=fac[q][:, 1, 1:2])
                    last.then_inc(z_ready, 1)
                elif kind == "h":
                    t, = a
                    img = i - back
                    act.wait_ge(corr_done, at(img, TILES, t + 1))
                    if not (isinstance(img, int) and img == 0):
                        act.wait_ge(picked, at(img, PICKS, picks_before(t // T, KMAX - 1, t % T) + 1 - PICKS))
                    act.activation(h[:, t, :], gen_ps[t % 2][:], ACT.Copy).then_inc(h_ready, 1)
                elif kind == "xn":
                    c, = a
                    if c == 0:
                        act.wait_ge(gn_step, at(i, 2 * GN_STEPS, GN_STEPS))
                        for n in range(2):
                            act.wait_ge(x_edge[n], at(i, 16, 16))
                    if not (isinstance(i, int) and i == 0 and c < XN_RING):
                        act.wait_ge(conv_done, at(i, CHUNKS, c - XN_RING + 1))
                    for tau in range(2):
                        src = 1 - tau
                        ps_, pd = slice(64 * src, 64 * src + 64), slice(64 * tau, 64 * tau + 64)
                        rows = slice(c * CP + tau, c * CP + tau + CP + 1)
                        sc, bi = fac[par][ps_, 0, 0:1], fac[par][ps_, 0, 1:2]
                        act.activation(xn[pd, c % XN_RING, :, 1:W + 1], xa[par][ps_, rows, :], ACT.Identity,
                                       scale=sc, bias=bi)
                        for to, of in ((0, W - 1), (W + 1, 0)):
                            last = act.activation(xn[pd, c % XN_RING, :, to:to + 1],
                                                  xa[par][ps_, rows, of:of + 1], ACT.Identity, scale=sc, bias=bi)
                    last.then_inc(xn_ready, 1)
                elif kind == "st":
                    if not (isinstance(i, int) and i == 0 and a[0] < PARTS):
                        statistics(act, i, par, *a)
                elif kind == "rt":
                    n, = a
                    act.wait_ge(gn_step, at(i, 2 * GN_STEPS, n * GN_STEPS + 5))
                    act.activation(gsc[:, 4:5], gsc[:, 3:4], ACT.Sqrt).then_inc(gn_root, 1)

            def period(i, par, loop=False):
                here = own, b, p = parts(i, loop)
                img = i - 1
                for s in range(SLOTS):
                    g, k, t = s // (KMAX * T), s // T % KMAX, s % T
                    if b:
                        if k > 0:
                            act.wait_ge(h_masked, at(img, LATER, (g * (KMAX - 1) + k - 1) * T + t + 1))
                        else:
                            act.wait_ge(h_ready, at(img, TILES, g * T + t + 1))
                        if not (isinstance(img, int) and img == 0 and s < 2):
                            act.wait_ge(atom_found, at(img, SLOTS, s - 1))
                        act.activation(score[s % 2][:], h[:, g * T + t, :], ACT.Abs).then_inc(score_ready, 1)
                    for what in SCALAR_PLAN.get(s, ()):
                        if here[lag(what, s)]:
                            extra(what, i, par, lag(what, s))

            periods(act, period)

        @block.vector
        def _(dve):
            def stop_until(sem_, value):
                dve.wait_ge(sem_, value)
                dve.sem_inc(vector_passed, 1)

            def extra(what, i, par, back):
                kind, *a = what
                if kind == "ca":
                    c, = a
                    dve.wait_ge(conv_done, at(i, CHUNKS, c + 1))
                    dve.wait_ge(xn_ready, at(i, CHUNKS, min(c + 2, CHUNKS)))
                    dst = xa[par][:, 1 + c * CP:1 + (c + 1) * CP, :]
                    dve.tensor_tensor(dst, conv_ps[c % 2][:], dst, ALU.add).then_inc(x1_ready, 1)
                elif kind == "ra":
                    g, d = a
                    img, q = i - back, par if back == 2 else 1 - par
                    ph, pj = divmod(d, PATCH)
                    half = PAIRS // GROUPS
                    dst = xa[q][:, 1 + g * half + ph:1 + (g + 1) * half:2, :]\
                        .rearrange("p h (w j) -> p j h w", j=PATCH)[:, pj]
                    dve.wait_ge(recon_done, at(img, GROUPS * ND, g * ND + d + 1))
                    dve.tensor_tensor(dst, gen_ps[d % 2][:].rearrange("p (h w) -> p h w", h=half // 2), dst, ALU.add)\
                        .then_inc(recon_added, 1)
                elif kind == "gn":
                    gn_part(i, par, *a)
                elif kind == "co":
                    coefficients(i - back, *a)
                elif kind == "ce":
                    g, t = a
                    img = i - back
                    n = g * T + t
                    for j in range(KMAX):
                        if t == 0 and j == 0:
                            dve.wait_ge(which_ready, at(img, GROUPS * KMAX, (g + 1) * KMAX))
                            dve.wait_ge(solve_step, at(img, GROUPS * SOLVE, (g + 1) * SOLVE))
                        if not (isinstance(img, int) and img == 0 and n == 0):
                            dve.wait_ge(ce_turned, at(img, TILES * KMAX, (n - 1) * KMAX + j + 1))
                        dve.tensor_scalar(ce[:, j, :], count[:], which[:, g, j, t:t + 1], xc[:, g, j, t:t + 1],
                                          ALU.is_equal, ALU.mult).then_inc(ce_ready, 1)

            def gn_part(i, par, n, part):
                base = n * GN_STEPS

                def after(step):
                    dve.wait_ge(gn_step, at(i, 2 * GN_STEPS, base + step))

                if part == 1:
                    dve.wait_ge(gn_sum, at(i, 4, 2 * n + 1))
                    dve.tensor_copy(gsc[:, 0:1], st_ps[:, 0:1]).then_inc(gn_step, 1)
                    after(2)
                    dve.tensor_tensor(gsc[:, 1:2], mv[:, n, 0:1], gsc[:, 0:1], ALU.subtract).then_inc(gn_step, 1)
                    after(3)
                    dve.scalar_tensor_tensor(gsc[:, 2:3], gsc[:, 1:2], gsc[:, 1:2], mv[:, n, 1:2], ALU.mult, ALU.add)\
                        .then_inc(gn_step, 1)
                    dve.wait_ge(gn_sum, at(i, 4, 2 * n + 2))
                    dve.tensor_scalar(gsc[:, 3:4], st_ps[:, 1:2], GN_EPS, None, ALU.add).then_inc(gn_step, 1)
                else:
                    stop_until(gn_root, at(i, 2, n + 1))
                    dve.reciprocal(gsc[:, 5:6], gsc[:, 4:5]).then_inc(gn_step, 1)
                    after(6)
                    dve.tensor_tensor(gsc[:, 6:7], gsc[:, 3:4], gsc[:, 5:6], ALU.mult).then_inc(gn_step, 1)
                    after(7)
                    dve.tensor_scalar(gsc[:, 7:8], gsc[:, 6:7], gsc[:, 4:5], 0.5, ALU.add, ALU.mult)\
                        .then_inc(gn_step, 1)
                    after(8)
                    dve.reciprocal(fac[par][:, n, 0:1], gsc[:, 7:8]).then_inc(gn_step, 1)
                    after(9)
                    dve.tensor_scalar(fac[par][:, n, 1:2], gsc[:, 0:1], -1.0, fac[par][:, n, 0:1], ALU.mult, ALU.mult)\
                        .then_inc(gn_step, 1)

            def pursuit_step(img, g, k, between):
                base = (g * KMAX + k) * T
                later = (g * (KMAX - 1) + k - 1) * T

                def search(t):
                    n = base + t
                    stop_until(score_ready, at(img, SLOTS, n + 1))
                    dve.max(top8[:, t, :], score[n % 2][:]).then_inc(top_found, 1)

                def locate(t):
                    n = base + t
                    if k:
                        dve.wait_ge(row_loaded[t], at(img, 16 * GROUPS * (KMAX - 1), 16 * (g * (KMAX - 1) + k)))
                    stop_until(top_found, at(img, SLOTS, n + 1))
                    dve.max_index(idx8[:, t, :], top8[:, t, :], score[n % 2][:]).then_inc(atom_found, 1)

                def one_hot(t):
                    dve.wait_ge(atom_found, at(img, SLOTS, base + t + 1))
                    if k == 0 and not (isinstance(img, int) and img == 0 and g == 0) and (1 - g, t) in AWAY:
                        dve.wait_ge(v_product, at(img, PICKS_AWAY, away_before(1 - g, t) + KMAX - 1
                                                  - (0 if g else PICKS_AWAY)))
                    dve.tensor_scalar(hot[:, t, :], count[:], idx8[:, t, 0:1], None, ALU.is_equal)\
                        .then_inc(hot_ready, 1)
                    if k == 0:
                        dve.tensor_scalar(mask[:, t, :], count[:], idx8[:, t, 0:1], None, ALU.not_equal)\
                            .then_inc(mask_ready, 1)

                def pick(t):
                    n = picks_before(g, k, t)
                    dve.wait_ge(hot_ready, at(img, SLOTS, base + t + 1))
                    for j in range(-1, picks(g, k, t) - 1):
                        if not (isinstance(img, int) and img == 0 and n < 4):
                            dve.wait_ge(picked, at(img, PICKS, n - 3))
                        dve.tensor_tensor_reduce(
                            out=junk[:, n % 4, :], in0=h[:, g * T + t, :] if j < 0 else u[:, t, j, :],
                            in1=hot[:, t, :], scale=1.0, scalar=0.0, op0=ALU.mult, op1=ALU.add,
                            accum_out=hsel[:, g, k, t:t + 1] if j < 0 else v[:, g, k, j, t:t + 1])\
                            .then_inc(picked, 1)
                        n += 1
                    if 0 < k < KMAX - 1:
                        dve.tensor_tensor(mask[:, t, :], mask[:, t, :], hot[:, t, :], ALU.subtract)\
                            .then_inc(mask_ready, 1)

                for t in range(T):
                    search(t)
                    if t > 0:
                        one_hot(t - 1)
                    locate(t)
                    if t > 0:
                        between(base + t - 1)
                        pick(t - 1)
                one_hot(T - 1)
                dve.tensor_copy(which[:, g, k, :], idx8[:, :, 0]).then_inc(which_ready, 1)
                between(base + T - 1)
                pick(T - 1)

            def factor_row(g, k, wait, step, n, squares, total, pivot):
                wait(n)
                dve.scalar_tensor_tensor(nl[:, g, k, 0:k, :], v[:, g, k, 0:k, :], -1.0, rd[:, g, 0:k, :],
                                         ALU.mult, ALU.mult).then_inc(step, 1)
                wait(n + 1)
                dst = squares[:, 0:k, :] if k > 1 else total[:].rearrange("p (a t) -> p a t", a=1)
                dve.tensor_tensor(dst, nl[:, g, k, 0:k, :], v[:, g, k, 0:k, :], ALU.mult).then_inc(step, 1)
                n += 2
                wait(n)
                if k > 1:
                    dve.tensor_reduce(total[:], squares[:, 0:k, :].rearrange("p j t -> p t j"), axis=AX.X, op=ALU.add)\
                        .then_inc(step, 1)
                    n += 1
                    wait(n)
                dve.tensor_scalar(pivot[:], total[:], 1.0, DIAG_EPS, ALU.add, ALU.max).then_inc(step, 1)
                wait(n + 1)
                dve.reciprocal(rd[:, g, k, :], pivot[:]).then_inc(step, 1)
                wait(n + 2)
                dve.scalar_tensor_tensor(na[:, g, k, :], hsel[:, g, k, :], -1.0, rd[:, g, k, :], ALU.mult, ALU.mult)\
                    .then_inc(step, 1)

            def algebra(img, g, k):
                dve.wait_ge(picked, at(img, PICKS, picks_before(g, k + 1)))
                if k == 0:
                    dve.tensor_scalar(na[:, g, 0, :], hsel[:, g, 0, :], -1.0, None, ALU.mult).then_inc(alg_step, 1)
                    return

                def wait(n):
                    dve.wait_ge(alg_step, at(img, GROUPS * ALG, n))

                factor_row(g, k, wait, alg_step, g * ALG + (1 + 6 * (k - 1) - 1 if k > 1 else 1), sq, ss, dd)

            def coefficients(img, g):
                n = g * SOLVE

                def wait(n):
                    dve.wait_ge(solve_step, at(img, GROUPS * SOLVE, n))

                dve.wait_ge(alg_step, at(img, GROUPS * ALG, (g + 1) * ALG))
                dve.wait_ge(picked, at(img, PICKS, picks_before(g + 1, 0)))
                if away_before(g + 1) > away_before(g):
                    stop_until(v_summed, at(img, PICKS_AWAY, away_before(g + 1)))
                factor_row(g, KMAX - 1, wait if g else lambda n: wait(n) if n else None, solve_step, n,
                           sq_last, ss_last, dd_last)
                n += 6
                wait(n)
                dve.tensor_scalar(xc[:, g], na[:, g], -1.0, None, ALU.mult).then_inc(solve_step, 1)
                n += 1
                for k in range(KMAX - 1, 0, -1):
                    wait(n)
                    dve.tensor_tensor(tmp[:, 0:k, :], nl[:, g, k, 0:k, :],
                                      xc[:, g, k:k + 1, :].to_broadcast([P, k, T]), ALU.mult).then_inc(solve_step, 1)
                    wait(n + 1)
                    dve.tensor_tensor(xc[:, g, 0:k, :], xc[:, g, 0:k, :], tmp[:, 0:k, :], ALU.add)\
                        .then_inc(solve_step, 1)
                    n += 2

            def project(img, g, k, between):
                rows = g * ROWS + T * sum(range(k))
                done = g * ALG + (1 if k == 0 else 6 * k)
                dve.wait_ge(alg_step, at(img, GROUPS * ALG, done))
                for pair in range(0, T, 2):
                    row = rows + pair * k
                    for j in range(k):
                        for t in (pair, pair + 1):
                            if j == 0:
                                dve.wait_ge(row_loaded[t],
                                            at(img, 16 * GROUPS * (KMAX - 1), 16 * (g * (KMAX - 1) + k + 1)))
                            else:
                                dve.wait_ge(row_step, at(img, GROUPS * ROWS, row + (j - 1) * 2 + t - pair + 1))
                            dve.scalar_tensor_tensor(u[:, t, k, :], u[:, t, j, :], nl[:, g, k, j, t:t + 1],
                                                     u[:, t, k, :], ALU.mult, ALU.add).then_inc(row_step, 1)
                    for t in (pair, pair + 1):
                        if k == 0:
                            dve.wait_ge(row_loaded[t], at(img, 16 * GROUPS * (KMAX - 1), 16 * (g * (KMAX - 1) + 1)))
                        else:
                            dve.wait_ge(row_step, at(img, GROUPS * ROWS, row + (k - 1) * 2 + t - pair + 1))
                        hh = h[:, g * T + t, :]
                        dve.scalar_tensor_tensor(hh, u[:, t, k, :], na[:, g, k, t:t + 1], hh, ALU.mult, ALU.add)\
                            .then_inc(h_updated, 1)
                    if pair == 0:
                        between((g * KMAX + k + 1) * T - 0.5)

            def period(i, par, loop=False):
                here = own, b, p = parts(i, loop)

                def between(s):
                    for what in VECTOR_PLAN.get(s, ()):
                        if here[lag(what, s)]:
                            extra(what, i, par, lag(what, s))

                for g in range(GROUPS):
                    for k in range(KMAX):
                        if not b:
                            for t in range(T):
                                between((g * KMAX + k) * T + t)
                            if k < KMAX - 1:
                                between((g * KMAX + k + 1) * T - 0.5)
                            continue
                        pursuit_step(i - 1, g, k, between)
                        if k < KMAX - 1:
                            algebra(i - 1, g, k)
                            project(i - 1, g, k, between)

            periods(dve, period)

        @block.tensor
        def _(pe):
            def turn(img, g):
                for t in range(T):
                    n = g * T + t
                    for j in range(KMAX):
                        pe.wait_ge(ce_ready, at(img, TILES * KMAX, n * KMAX + j + 1))
                        if j == 0 and not (isinstance(img, int) and img == 0 and n == 0):
                            pe.wait_ge(ct_ready, at(img, TILES, n))
                        for a in range(NA):
                            last = pe.matmul(ct_ps[:, a, :], ce[:, j, a * P:(a + 1) * P], ident[:], is_transpose=True,
                                             start=(j == 0 and a == 0), stop=(j == KMAX - 1), skip_group_check=True)
                        last.then_inc(ce_turned, 1)

            def recon(img, g, between=lambda done: None):
                for d in range(ND):
                    if d == 0:
                        pe.wait_ge(ct_ready, at(img, TILES, (g + 1) * T))
                    if d < 2:
                        after = img + 1 if g else img
                        pe.wait_ge(h_ready, at(after, TILES, (AHEAD if g else TILES) - 1 + d)
                                   if not (isinstance(after, int) and after >= images) else at(images - 1, TILES, TILES))
                    else:
                        pe.wait_ge(recon_added, at(img, GROUPS * ND, g * ND + d - 1))
                    for a in range(NA):
                        last = pe.matmul(gen_ps[d % 2][:], dt_[:, a, d, :], ct[:, a, :], start=(a == 0), stop=(a == NA - 1))
                    last.then_inc(recon_done, 1)
                    between(d + 1)

            def correlate(img, tiles):
                for t in tiles:
                    pe.wait_ge(z_ready, at(img, TILES, t + 1))
                    first = isinstance(img, int) and img == 0
                    if t < 2 and not first:
                        pe.wait_ge(recon_added, at(img, GROUPS * ND, t - 1 - ND))
                    elif t >= AHEAD and not first:
                        pe.wait_ge(recon_added, at(img, GROUPS * ND, t - AHEAD - 1))
                    elif t >= 2:
                        pe.wait_ge(h_ready, at(img, TILES, t - 1))
                    for d in range(ND):
                        last = pe.matmul(gen_ps[t % 2][:], z[:, t % 2, d // PATCH, d % PATCH, :], dn[:, d, :],
                                         start=(d == 0), stop=(d == ND - 1))
                    last.then_inc(corr_done, 1)

            def average(i, n):
                pe.wait_ge(gn_step, at(i, 2 * GN_STEPS, n * GN_STEPS + 1))
                pe.matmul(st_ps[:, 0:1], avg[:], mv[:, n, 0:1], start=True, stop=True).then_inc(gn_sum, 1)
                pe.wait_ge(gn_step, at(i, 2 * GN_STEPS, n * GN_STEPS + 4))
                pe.matmul(st_ps[:, 1:2], avg[:], gsc[:, 2:3], start=True, stop=True).then_inc(gn_sum, 1)

            def convolve(i, between):
                for c in range(CHUNKS):
                    pe.wait_ge(xn_ready, at(i, CHUNKS, c + 1))
                    if not (isinstance(i, int) and i == 0 and c < 2):
                        pe.wait_ge(x1_ready, at(i, CHUNKS, c - 1))
                    for m in range(2 * TAPS):
                        rows, tap = divmod(m, TAPS)
                        last = pe.matmul(conv_ps[c % 2][:], wc[:, m, :], xn[:, c % XN_RING, rows:rows + CP, tap:tap + W],
                                         start=(m == 0), stop=(m == 2 * TAPS - 1))
                    last.then_inc(conv_done, 1)
                    between(c + 1)

            def period(i, par, loop=False):
                own, b, p = parts(i, loop)
                if p:
                    turn(i - 2, 1)
                    recon(i - 2, 1)
                if b:
                    correlate(i - 1, range(AHEAD, TILES))
                if own:
                    average(i, 0)
                    convolve(i, lambda done: turn(i - 1, 0) if b and done == TURN_AFTER else None)
                elif b:
                    turn(i - 1, 0)
                if b:
                    recon(i - 1, 0, lambda done: average(i, 1) if own and done == AVERAGE_AFTER else None)
                elif own:
                    average(i, 1)
                if own:
                    correlate(i, range(AHEAD))

            periods(pe, period)


def setup(nc, ctx, sem, w_taps, atoms, ident_in, avg_in, gram, dn, dt_, wc, h, u, count, ident, avg,
          rd, gen_ps, ct_ps, st_ps, first_loads, first_statistics):
    atoms_in = sem("atoms_in")
    consts_in = sem("consts_in")
    taps_in = sem("taps_in")
    cleared = sem("cleared")
    squared = sem("squared")
    summed = sem("summed")
    rooted = sem("rooted")
    inverse = sem("inverse")
    scaled = sem("scaled")
    gram_done = sem("gram_done")
    gram_copied = sem("gram_copied")
    gram_out = sem("gram_out")
    turned = sem("turned")
    turned_copied = sem("turned_copied")
    counted = sem("counted")
    ones = h[:, 7, 0:P]
    with nc.Block() as block:
        @block.sync
        def _(sp):
            sp.dma_start(dn[:], atoms).then_inc(atoms_in, 16)
            sp.dma_start(ident[:], ident_in).then_inc(consts_in, 16)
            sp.dma_start(avg[:], avg_in).then_inc(consts_in, 16)
            sp.wait_ge(cleared, 1)
            for row in range(2):
                for tau in range(2):
                    for s in range(2):
                        a = 2 * row + tau - s
                        if 0 <= a < TAPS:
                            sp.dma_start(wc[64 * tau:64 * tau + 64, row * TAPS:(row + 1) * TAPS, 64 * s:64 * s + 64],
                                         w_taps[:, a, :, :]).then_inc(taps_in, 16)
            first_loads(sp)
            sp.wait_ge(taps_in, 16 * 6)
            for a in range(NA):
                sp.wait_ge(gram_copied, 2 * a + 2)
                sp.dma_start(gram[a * P:(a + 1) * P, :], u[:, a, 0, :]).then_inc(gram_out, 16)
            sp.wait_ge(gram_out, 16 * NA)

        @block.gpsimd
        def _(pool):
            pool.iota(count[:], [[1, ATOMS]], base=0, channel_multiplier=0,
                      allow_small_or_imprecise_dtypes=True).then_inc(counted, 1)
            pool.wait_ge(counted, 1)

        @block.scalar
        def _(act):
            act.wait_ge(atoms_in, 16)
            for d in range(ND):
                act.activation(u[:, d // 2, d % 2, :], dn[:, d, :], ACT.Square).then_inc(squared, 1)
            act.wait_ge(summed, 1)
            act.activation(h[:, 0, :], st_ps[:], ACT.Sqrt).then_inc(rooted, 1)
            first_statistics(act)
            for n in range(2 * NA):
                act.wait_ge(turned, n + 1)
                a, half = divmod(n, 2)
                act.activation(dt_[:, a, half * 4:half * 4 + 4, :], ct_ps[:], ACT.Copy).then_inc(turned_copied, 1)

        @block.vector
        def _(dve):
            dve.memset(wc[:], 0.0).then_inc(cleared, 1)
            dve.memset(ones, 1.0).then_inc(cleared, 1)
            dve.memset(rd[:], 1.0)
            dve.wait_ge(rooted, 1)
            dve.tensor_scalar(h[:, 1, :], h[:, 0, :], 1e-20, None, ALU.max).then_inc(inverse, 1)
            dve.wait_ge(inverse, 1)
            dve.reciprocal(h[:, 2, :], h[:, 1, :]).then_inc(inverse, 1)
            dve.wait_ge(inverse, 2)
            dve.tensor_tensor(h[:, 3, :], st_ps[:], h[:, 2, :], ALU.mult).then_inc(inverse, 1)
            dve.wait_ge(inverse, 3)
            dve.tensor_tensor(h[:, 4, :], h[:, 3, :], h[:, 1, :], ALU.add).then_inc(inverse, 1)
            dve.wait_ge(inverse, 4)
            dve.tensor_scalar(h[:, 5, :], h[:, 4, :], 0.5, NORM_EPS, ALU.mult, ALU.add).then_inc(inverse, 1)
            dve.wait_ge(inverse, 5)
            dve.reciprocal(h[:, 6, :], h[:, 5, :]).then_inc(inverse, 1)
            dve.wait_ge(inverse, 6)
            for d in range(ND):
                dve.tensor_tensor(dn[:, d, :], dn[:, d, :], h[:, 6, :], ALU.mult).then_inc(scaled, 1)
            dve.wait_ge(consts_in, 32)
            for a in range(NA):
                dve.wait_ge(gram_done, a + 1)
                dve.tensor_copy(u[:, a, 0, :], gen_ps[a % 2][:]).then_inc(gram_copied, 1)
                dve.wait_ge(gram_copied, 2 * a + 1)
                diag = u[:, a, 0, a * P:(a + 1) * P]
                dve.scalar_tensor_tensor(diag, ident[:], DIAG_EPS, diag, ALU.mult, ALU.add).then_inc(gram_copied, 1)

        @block.tensor
        def _(pe):
            pe.wait_ge(cleared, 2)
            for d in range(ND):
                pe.wait_ge(squared, d + 1)
                last = pe.matmul(st_ps[:], ones, u[:, d // 2, d % 2, :], start=(d == 0), stop=(d == ND - 1))
            last.then_inc(summed, 1)
            pe.wait_ge(scaled, ND)
            for a in range(NA):
                if a >= 2:
                    pe.wait_ge(gram_copied, 2 * a - 3)
                for d in range(ND):
                    last = pe.matmul(gen_ps[a % 2][:], dn[:, d, a * P:(a + 1) * P], dn[:, d, :],
                                     start=(d == 0), stop=(d == ND - 1))
                last.then_inc(gram_done, 1)
            pe.wait_ge(consts_in, 32)
            for n in range(2 * NA):
                a, half = divmod(n, 2)
                if n >= 1:
                    pe.wait_ge(turned_copied, n)
                for m in range(4):
                    last = pe.transpose(ct_ps[:, m, :], dn[:, half * 4 + m, a * P:(a + 1) * P], ident[:])
                last.then_inc(turned, 1)


def kernel(x, L0_conv_weight, L1_conv_dictionary):
    import concourse.bacc as bacc
    from concourse.bass_utils import run_bass_kernel_spmd

    x, weight, dictionary = (np.asarray(a) for a in (x, L0_conv_weight, L1_conv_dictionary))
    images = x.shape[0]
    arrays = {
        "x_pairs": np.ascontiguousarray(x.reshape(images, CIN, PAIRS, 2, W).transpose(0, 3, 1, 2, 4))
                     .reshape(images, P, PAIRS, W),
        "w_taps": np.ascontiguousarray(weight.transpose(1, 2, 3, 0)),
        "atoms": np.ascontiguousarray(dictionary.reshape(CIN, 2, 2, PATCH, ATOMS).transpose(2, 0, 1, 3, 4))
                   .reshape(P, ND, ATOMS),
        "ident_in": np.eye(P, dtype=np.float32),
        "avg_in": np.kron(np.ones((2, 2)), np.kron(np.eye(CIN // 2), np.full((2, 2), 0.25))).astype(np.float32),
    }
    nc = bacc.Bacc("TRN2", target_bir_lowering=False, num_devices=1)
    ins = [nc.dram_tensor(n, a.shape, mybir.dt.from_np(a.dtype), kind="ExternalInput").ap() for n, a in arrays.items()]
    y = nc.dram_tensor("y_pairs", (images, P, PAIRS, W), F32, kind="ExternalOutput").ap()
    preact_conv_pursuit(nc, *ins, y)
    r = run_bass_kernel_spmd(nc, [arrays], core_ids=[0])
    got = r.results[0]["y_pairs"]
    return np.ascontiguousarray(got.reshape(images, 2, CIN, PAIRS, W).transpose(0, 2, 3, 1, 4)).reshape(x.shape)
```
